# Optimizing a Trainium2 kernel written in Bass

```python
import numpy as np
import jax
import jax.numpy as jnp

def _softmax(x, axis=-1):
    return jax.nn.softmax(x, axis=axis)

def _gelu(x):
    return jax.nn.gelu(x, approximate=True)

def _silu(x):
    return jax.nn.silu(x)

def _sigmoid(x):
    return jax.nn.sigmoid(x)

def _layernorm(x, axis=-1, eps=1e-05):
    m = jnp.mean(x, axis=axis, keepdims=True)
    v = jnp.var(x, axis=axis, keepdims=True)
    return (x - m) / jnp.sqrt(v + eps)

def _scatter_add(tgt, idx, src, axis=0):
    return tgt.at[idx].add(src)

def _segment_sum(src, seg, n):
    return jax.ops.segment_sum(src, seg, n)
kernel_name = 'mk_rec_standalone_d1_rec_r8_7784cc'

def setup_inputs(seed: int=0):
    np.random.seed(seed)
    _w = jnp.asarray

    def _rec_inputs():
        import jax
        import jax.numpy as jnp
        _rk = jax.random.key(seed)
        r_dense_input = jax.random.uniform(jax.random.fold_in(_rk, 1), (2048, 13), jnp.float32, 0.0, 0.999986)
        r_sparse_input = jnp.stack([jax.random.randint(jax.random.fold_in(jax.random.fold_in(_rk, 2), 0), (2048,), 0, 1250, jnp.int32), jax.random.randint(jax.random.fold_in(jax.random.fold_in(_rk, 2), 1), (2048,), 0, 9996, jnp.int32), jax.random.randint(jax.random.fold_in(jax.random.fold_in(_rk, 2), 2), (2048,), 0, 1250, jnp.int32), jax.random.randint(jax.random.fold_in(jax.random.fold_in(_rk, 2), 3), (2048,), 0, 1250, jnp.int32), jax.random.randint(jax.random.fold_in(jax.random.fold_in(_rk, 2), 4), (2048,), 0, 1250, jnp.int32), jax.random.randint(jax.random.fold_in(jax.random.fold_in(_rk, 2), 5), (2048,), 0, 1250, jnp.int32), jax.random.randint(jax.random.fold_in(jax.random.fold_in(_rk, 2), 6), (2048,), 0, 9999, jnp.int32), jax.random.randint(jax.random.fold_in(jax.random.fold_in(_rk, 2), 7), (2048,), 0, 1250, jnp.int32), jax.random.randint(jax.random.fold_in(jax.random.fold_in(_rk, 2), 8), (2048,), 0, 1250, jnp.int32), jax.random.randint(jax.random.fold_in(jax.random.fold_in(_rk, 2), 9), (2048,), 1, 1250, jnp.int32), jax.random.randint(jax.random.fold_in(jax.random.fold_in(_rk, 2), 10), (2048,), 1, 9998, jnp.int32), jax.random.randint(jax.random.fold_in(jax.random.fold_in(_rk, 2), 11), (2048,), 2, 1250, jnp.int32), jax.random.randint(jax.random.fold_in(jax.random.fold_in(_rk, 2), 12), (2048,), 0, 9999, jnp.int32), jax.random.randint(jax.random.fold_in(jax.random.fold_in(_rk, 2), 13), (2048,), 1, 9998, jnp.int32), jax.random.randint(jax.random.fold_in(jax.random.fold_in(_rk, 2), 14), (2048,), 0, 1250, jnp.int32), jax.random.randint(jax.random.fold_in(jax.random.fold_in(_rk, 2), 15), (2048,), 0, 1250, jnp.int32), jax.random.randint(jax.random.fold_in(jax.random.fold_in(_rk, 2), 16), (2048,), 2, 9999, jnp.int32), jax.random.randint(jax.random.fold_in(jax.random.fold_in(_rk, 2), 17), (2048,), 1, 1250, jnp.int32), jax.random.randint(jax.random.fold_in(jax.random.fold_in(_rk, 2), 18), (2048,), 1, 1250, jnp.int32), jax.random.randint(jax.random.fold_in(jax.random.fold_in(_rk, 2), 19), (2048,), 1, 1250, jnp.int32), jax.random.randint(jax.random.fold_in(jax.random.fold_in(_rk, 2), 20), (2048,), 0, 1250, jnp.int32), jax.random.randint(jax.random.fold_in(jax.random.fold_in(_rk, 2), 21), (2048,), 1, 1250, jnp.int32), jax.random.randint(jax.random.fold_in(jax.random.fold_in(_rk, 2), 22), (2048,), 0, 1250, jnp.int32), jax.random.randint(jax.random.fold_in(jax.random.fold_in(_rk, 2), 23), (2048,), 1, 1250, jnp.int32), jax.random.randint(jax.random.fold_in(jax.random.fold_in(_rk, 2), 24), (2048,), 2, 1250, jnp.int32), jax.random.randint(jax.random.fold_in(jax.random.fold_in(_rk, 2), 25), (2048,), 2, 1250, jnp.int32)], axis=1)
        return (r_dense_input, r_sparse_input)
    r_dense_input, r_sparse_input = _rec_inputs()

    def _L0_rec_setup():
        import jax, jax.numpy as jnp
        import numpy as np
        B = 1024
        N_DENSE = 13
        N_SPARSE = 26
        FEAT_NUM = 1250
        E = 64
        H = 8
        ATT_LAYERS = 3
        IN_DIM = (N_DENSE + N_SPARSE) * E
        HIDDEN = [IN_DIM, 1024, 512, 256]

        def _dnn(x, ws, bs):
            for w, b in zip(ws, bs):
                x = jax.nn.relu(x @ w.T + b)
            return x

        def _interact(x, wq, wv, wr):
            b, f, e = x.shape
            d = e // H
            q = jnp.einsum('bfe,oe->bfo', x, wq).reshape(b, f, H, d)
            v = jnp.einsum('bfe,oe->bfo', x, wv).reshape(b, f, H, d)
            scores = jnp.einsum('bihd,bjhd->bhij', q, q) / d ** 0.5
            attn = jax.nn.softmax(scores, axis=-1)
            out = jnp.einsum('bhij,bjhd->bihd', attn, v).reshape(b, f, e)
            return jax.nn.relu(out + jnp.einsum('bfe,oe->bfo', x, wr))
        key = jax.random.key(seed)
        ks = iter(jax.random.split(key, 40))
        s = 0.02
        inp = {'dense_input': jax.random.uniform(next(ks), (B, N_DENSE), dtype=jnp.float32), 'sparse_input': jax.random.randint(next(ks), (B, N_SPARSE), 0, FEAT_NUM, dtype=jnp.int32).astype(jnp.int64), 'dense_embed': jax.random.normal(next(ks), (N_DENSE, E), dtype=jnp.float32) * s, 'sparse_embed': jax.random.normal(next(ks), (N_SPARSE, FEAT_NUM, E), dtype=jnp.float32) * s, 'lin_w': jax.random.normal(next(ks), (1, IN_DIM), dtype=jnp.float32) * s, 'lin_b': jnp.zeros((1,), dtype=jnp.float32)}
        for pre in ('dnn', 'att_dnn'):
            for i in range(3):
                inp[f'{pre}_w{i}'] = jax.random.normal(next(ks), (HIDDEN[i + 1], HIDDEN[i]), dtype=jnp.float32) * s
                inp[f'{pre}_b{i}'] = jnp.zeros((HIDDEN[i + 1],), dtype=jnp.float32)
            inp[f'{pre}_out_w'] = jax.random.normal(next(ks), (1, HIDDEN[-1]), dtype=jnp.float32) * s
            inp[f'{pre}_out_b'] = jnp.zeros((1,), dtype=jnp.float32)
        inp['att_wq'] = jax.random.normal(next(ks), (ATT_LAYERS, E, E), dtype=jnp.float32) * s
        inp['att_wv'] = jax.random.normal(next(ks), (ATT_LAYERS, E, E), dtype=jnp.float32) * s
        inp['att_wr'] = jax.random.normal(next(ks), (ATT_LAYERS, E, E), dtype=jnp.float32) * s
        return inp
    _L0_rec_all = _L0_rec_setup()
    _L0_rec_in = {k: v for k, v in _L0_rec_all.items() if k in ('dense_embed', 'sparse_embed', 'lin_w', 'lin_b', 'dnn_w0', 'dnn_b0', 'dnn_w1', 'dnn_b1', 'dnn_w2', 'dnn_b2', 'dnn_out_w', 'dnn_out_b', 'att_dnn_w0', 'att_dnn_b0', 'att_dnn_w1', 'att_dnn_b1', 'att_dnn_w2', 'att_dnn_b2', 'att_dnn_out_w', 'att_dnn_out_b', 'att_wq', 'att_wv', 'att_wr')}
    del _L0_rec_all
    return {'r_dense_input': r_dense_input, 'r_sparse_input': r_sparse_input, 'L0_rec_dense_embed': _L0_rec_in['dense_embed'], 'L0_rec_sparse_embed': _L0_rec_in['sparse_embed'], 'L0_rec_lin_w': _L0_rec_in['lin_w'], 'L0_rec_lin_b': _L0_rec_in['lin_b'], 'L0_rec_dnn_w0': _L0_rec_in['dnn_w0'], 'L0_rec_dnn_b0': _L0_rec_in['dnn_b0'], 'L0_rec_dnn_w1': _L0_rec_in['dnn_w1'], 'L0_rec_dnn_b1': _L0_rec_in['dnn_b1'], 'L0_rec_dnn_w2': _L0_rec_in['dnn_w2'], 'L0_rec_dnn_b2': _L0_rec_in['dnn_b2'], 'L0_rec_dnn_out_w': _L0_rec_in['dnn_out_w'], 'L0_rec_dnn_out_b': _L0_rec_in['dnn_out_b'], 'L0_rec_att_dnn_w0': _L0_rec_in['att_dnn_w0'], 'L0_rec_att_dnn_b0': _L0_rec_in['att_dnn_b0'], 'L0_rec_att_dnn_w1': _L0_rec_in['att_dnn_w1'], 'L0_rec_att_dnn_b1': _L0_rec_in['att_dnn_b1'], 'L0_rec_att_dnn_w2': _L0_rec_in['att_dnn_w2'], 'L0_rec_att_dnn_b2': _L0_rec_in['att_dnn_b2'], 'L0_rec_att_dnn_out_w': _L0_rec_in['att_dnn_out_w'], 'L0_rec_att_dnn_out_b': _L0_rec_in['att_dnn_out_b'], 'L0_rec_att_wq': _L0_rec_in['att_wq'], 'L0_rec_att_wv': _L0_rec_in['att_wv'], 'L0_rec_att_wr': _L0_rec_in['att_wr']}

def reference(r_dense_input, r_sparse_input, L0_rec_dense_embed, L0_rec_sparse_embed, L0_rec_lin_w, L0_rec_lin_b, L0_rec_dnn_w0, L0_rec_dnn_b0, L0_rec_dnn_w1, L0_rec_dnn_b1, L0_rec_dnn_w2, L0_rec_dnn_b2, L0_rec_dnn_out_w, L0_rec_dnn_out_b, L0_rec_att_dnn_w0, L0_rec_att_dnn_b0, L0_rec_att_dnn_w1, L0_rec_att_dnn_b1, L0_rec_att_dnn_w2, L0_rec_att_dnn_b2, L0_rec_att_dnn_out_w, L0_rec_att_dnn_out_b, L0_rec_att_wq, L0_rec_att_wv, L0_rec_att_wr):
    import jax
    import jax.numpy as jnp

    def _L0_rec_ref(dense_input, sparse_input, dense_embed, sparse_embed, lin_w, lin_b, dnn_w0, dnn_b0, dnn_w1, dnn_b1, dnn_w2, dnn_b2, dnn_out_w, dnn_out_b, att_dnn_w0, att_dnn_b0, att_dnn_w1, att_dnn_b1, att_dnn_w2, att_dnn_b2, att_dnn_out_w, att_dnn_out_b, att_wq, att_wv, att_wr):
        import jax, jax.numpy as jnp
        import numpy as np
        B = 1024
        N_DENSE = 13
        N_SPARSE = 26
        FEAT_NUM = 1250
        E = 64
        H = 8
        ATT_LAYERS = 3
        IN_DIM = (N_DENSE + N_SPARSE) * E
        HIDDEN = [IN_DIM, 1024, 512, 256]

        def _dnn(x, ws, bs):
            for w, b in zip(ws, bs):
                x = jax.nn.relu(x @ w.T + b)
            return x

        def _interact(x, wq, wv, wr):
            b, f, e = x.shape
            d = e // H
            q = jnp.einsum('bfe,oe->bfo', x, wq).reshape(b, f, H, d)
            v = jnp.einsum('bfe,oe->bfo', x, wv).reshape(b, f, H, d)
            scores = jnp.einsum('bihd,bjhd->bhij', q, q) / d ** 0.5
            attn = jax.nn.softmax(scores, axis=-1)
            out = jnp.einsum('bhij,bjhd->bihd', attn, v).reshape(b, f, e)
            return jax.nn.relu(out + jnp.einsum('bfe,oe->bfo', x, wr))
        b = dense_input.shape[0]
        dense_part = dense_input[:, :, None] * dense_embed[None]
        sparse_part = sparse_embed[jnp.arange(N_SPARSE)[None, :], sparse_input]
        all_input = jnp.concatenate([dense_part, sparse_part], axis=1).reshape(b, -1)
        linear_out = all_input @ lin_w.T + lin_b
        dnn_out = _dnn(all_input, (dnn_w0, dnn_w1, dnn_w2), (dnn_b0, dnn_b1, dnn_b2))
        dnn_out = dnn_out @ dnn_out_w.T + dnn_out_b
        att = all_input.reshape(b, -1, E)
        for i in range(ATT_LAYERS):
            att = _interact(att, att_wq[i], att_wv[i], att_wr[i])
        att_flat = att.reshape(b, -1)
        att_out = _dnn(att_flat, (att_dnn_w0, att_dnn_w1, att_dnn_w2), (att_dnn_b0, att_dnn_b1, att_dnn_b2))
        att_out = att_out @ att_dnn_out_w.T + att_dnn_out_b
        return jax.nn.sigmoid(linear_out + dnn_out + att_out).squeeze()
    y = _L0_rec_ref(r_dense_input, r_sparse_input, L0_rec_dense_embed, L0_rec_sparse_embed, L0_rec_lin_w, L0_rec_lin_b, L0_rec_dnn_w0, L0_rec_dnn_b0, L0_rec_dnn_w1, L0_rec_dnn_b1, L0_rec_dnn_w2, L0_rec_dnn_b2, L0_rec_dnn_out_w, L0_rec_dnn_out_b, L0_rec_att_dnn_w0, L0_rec_att_dnn_b0, L0_rec_att_dnn_w1, L0_rec_att_dnn_b1, L0_rec_att_dnn_w2, L0_rec_att_dnn_b2, L0_rec_att_dnn_out_w, L0_rec_att_dnn_out_b, L0_rec_att_wq, L0_rec_att_wv, L0_rec_att_wr)
    return y

_drawn_inputs = setup_inputs


def setup_inputs(seed=0):
    import zlib

    import numpy as np

    out = dict(_drawn_inputs(seed))
    spreads = {'L0_rec_dnn_b0': (0.0, 0.8),
     'L0_rec_dnn_b1': (0.0, 0.8),
     'L0_rec_dnn_b2': (0.0, 0.513),
     'L0_rec_att_dnn_b0': (0.0, 0.8),
     'L0_rec_att_dnn_b1': (0.0, 0.8),
     'L0_rec_att_dnn_b2': (0.0, 0.8)}
    factors = {'r_dense_input': 8.0,
     'L0_rec_dense_embed': 8.0,
     'L0_rec_sparse_embed': 7.446,
     'L0_rec_lin_w': 7.617,
     'L0_rec_dnn_w0': 8.0,
     'L0_rec_dnn_w1': 8.0,
     'L0_rec_dnn_w2': 8.0,
     'L0_rec_dnn_out_w': 2.699,
     'L0_rec_att_dnn_w0': 8.0,
     'L0_rec_att_dnn_w1': 64.0,
     'L0_rec_att_dnn_w2': 8.0,
     'L0_rec_att_dnn_out_w': 8.0,
     'L0_rec_att_wq': 8.0,
     'L0_rec_att_wv': 8.0,
     'L0_rec_att_wr': 8.0}
    for name, (base, spread) in spreads.items():
        noise = np.random.default_rng([zlib.crc32(name.encode()), seed]).standard_normal(out[name].shape)
        drawn = base * np.exp(spread * noise) if base else spread * noise
        out[name] = jnp.asarray(drawn.astype(out[name].dtype))
    for name, factor in factors.items():
        out[name] = (out[name] * factor).astype(out[name].dtype)
    return out
```

```python
from contextlib import ExitStack

import numpy as np
import concourse.bass as bass
from concourse import mybir

F32 = mybir.dt.float32
I32 = mybir.dt.int32
ALU = mybir.AluOpType
ACT = mybir.ActivationFunctionType
AX_X = mybir.AxisListType.X

P = 128
E = 64
H = 8
D = 8
HALVES = 2
QUADS = 4
LAYERS = 3
PACK = 3
LANES = 4
GROUPS = 8
CHUNK = GROUPS * PACK
STREAMS = 2
STEP = STREAMS * CHUNK
BATCH = 512


def constants(F):
    T = PACK * F
    p = np.arange(P)
    lane = (p // D) % LANES
    c = {}
    c["ident"] = np.eye(P)
    c["same_sample"] = (lane[:, None] == lane[None, :]) & (lane[:, None] < PACK)
    out_v = (np.arange(H * PACK * D) // D) % PACK
    c["same_sample_v"] = lane[:, None] == out_v[None, :]
    c["is_sample"] = lane[:, None] == np.arange(PACK)[None, :]
    c["is_quad"] = (p // 32)[:, None] == np.arange(QUADS)[None, :]
    c["minus_diag"] = -1.0 * ((p % F)[:, None] == np.arange(F)[None, :])
    ones = (p // F)[:, None] == (p // F)[None, :]
    c["ones_block"] = ones
    sample = p // F
    v = np.zeros((P, D))
    for s in range(PACK):
        v[:, s] = sample == s
    v[:, PACK] = sample == 0
    c["sum_columns"] = v
    return {k: np.ascontiguousarray(a, dtype=np.float32) for k, a in c.items()}


def build_kernel(nc, a, out):
    B, ND = a["dense"].shape
    NS = a["sparse"].shape[1]
    ROWS = a["table"].shape[0] // NS
    F = ND + NS
    K0 = F * E
    T = PACK * F
    TILES = B // P
    H1, H2, H3 = a["dnn_w0"].shape[1], a["dnn_w1"].shape[1], a["dnn_w2"].shape[1]
    STEPS = -(-B // STEP)
    KC = -(-K0 // P)
    HF = GROUPS * F
    HC = QUADS * F
    NV = H * PACK * D
    SCALE = float(D) ** -0.5
    X_ROWS = (STEPS + 1) * STEP
    x_dram = nc.dram_tensor("x_rows", (X_ROWS, K0), F32, kind="Internal").ap()
    att_dram = nc.dram_tensor("att_rows", (STEPS * STEP + CHUNK, K0), F32, kind="Internal").ap()

    with ExitStack() as whole:
        sb = lambda name, shape, dt=F32: whole.enter_context(nc.sbuf_tensor(name, shape, dt))
        sem = lambda name: whole.enter_context(nc.semaphore(name))
        w0 = sb("w0", [P, KC, H1])
        w1 = sb("w1", [P, H1 // P, H2])
        w2 = sb("w2", [P, H2 // P, H3])
        w3 = sb("w3", [P, H3 // P])
        b0 = sb("b0", [P, H1 // P])
        b1 = sb("b1", [P, H2 // P])
        b2 = sb("b2", [P, H3 // P])
        lin_sum = sb("lin_sum", [P, TILES])
        dnn_sum = sb("dnn_sum", [P, TILES])
        att_sum = sb("att_sum", [P, TILES])
        ident = sb("ident", [P, P])
        weights_in = sem("weights_in")

        def load_weights(eng, pre):
            full = K0 // P
            w0_rows = a[pre + "_w0"]
            step = 5
            n = 0
            for c in range(0, full, step):
                k = min(step, full - c)
                eng.dma_start(w0[:, c:c + k, :], w0_rows[c * P:(c + k) * P, :].rearrange("(c p) n -> p c n", p=P)) \
                   .then_inc(weights_in, 16)
                n += 1
            if K0 % P:
                eng.dma_start(w0[0:K0 % P, full, :], w0_rows[full * P:K0, :]).then_inc(weights_in, 16)
                n += 1
            for dst, name in ((w1, "_w1"), (w2, "_w2")):
                eng.dma_start(dst[:], a[pre + name].rearrange("(c p) n -> p c n", p=P)).then_inc(weights_in, 16)
                n += 1
            for dst, name in ((w3, "_out_w"), (b0, "_b0"), (b1, "_b1"), (b2, "_b2")):
                eng.dma_start(dst[:], a[pre + name]).then_inc(weights_in, 16)
                n += 1
            return 16 * n

        def clear(sems):
            with nc.Block() as block:
                @block.sync
                def _(sp):
                    for s in sems:
                        sp.sem_clear(s)

        WEIGHTS = gather_stage(nc, a, x_dram, lin_sum, ident, load_weights, clear, B, ND, NS, ROWS, F, K0, TILES,
                               X_ROWS)
        dnn_stage(nc, x_dram, 0, dnn_sum, ident, (w0, w1, w2, w3), (b0, b1, b2), weights_in, WEIGHTS, clear,
                  B, K0, H1, H2, H3)
        clear([weights_in])
        attention_stage(nc, a, x_dram, att_dram, ident, load_weights, clear, F, K0, STEPS)
        dnn_stage(nc, att_dram, CHUNK, att_sum, ident, (w0, w1, w2, w3), (b0, b1, b2), weights_in, WEIGHTS, clear,
                  B, K0, H1, H2, H3)
        finish_stage(nc, a, out, lin_sum, dnn_sum, att_sum, ident, TILES)


def gather_stage(nc, a, x_dram, lin_sum, ident, load_weights, clear, B, ND, NS, ROWS, F, K0, TILES, X_ROWS):
    with ExitStack() as ctx:
        sb = lambda name, shape, dt=F32: ctx.enter_context(nc.sbuf_tensor(name, shape, dt))
        sem = lambda name: ctx.enter_context(nc.semaphore(name))
        idx_in = sb("idx_in", [P, TILES, NS], I32)
        idx_f = sb("idx_f", [P, TILES, NS])
        wrap = sb("wrap", [P, TILES, NS])
        rows = sb("rows", [P, TILES, NS], I32)
        rows_now = sb("rows_now", [P, 2, NS], I32)
        base = sb("table_base_sb", [P, NS])
        dense = sb("dense_sb", [P, TILES, ND])
        embed = sb("embed", [P, ND, E])
        lin_w = sb("lin_w_sb", [P, K0])
        junk = sb("junk", [P, K0])
        lin_now = sb("lin_now", [P, 2])
        x = sb("x_gather", [P, 2, K0])
        small_in = sem("small_in")
        zeros_ready = sem("zeros_ready")
        zeros_stored = sem("zeros_stored")
        idx_step = sem("idx_step")
        rows_ready = sem("rows_ready")
        gathered = [sem(f"gathered{j}") for j in range(2)]
        x_ready = sem("x_ready")
        lin_ready = sem("lin_ready")
        x_stored = sem("x_stored")
        count = []
        with nc.Block() as block:
            @block.sync
            def _(sp):
                sp.dma_start(idx_in[:], a["sparse"].rearrange("(t p) n -> p t n", p=P)).then_inc(small_in, 16)
                sp.dma_start(dense[:], a["dense"].rearrange("(t p) n -> p t n", p=P)).then_inc(small_in, 16)
                sp.dma_start(base[:], a["table_base"].partition_broadcast(P)).then_inc(small_in, 16)
                sp.dma_start(embed[:].rearrange("p f e -> p (f e)"), a["embed"].partition_broadcast(P)) \
                  .then_inc(small_in, 16)
                sp.dma_start(lin_w[:], a["lin_w"].partition_broadcast(P)).then_inc(small_in, 16)
                sp.dma_start(ident[:], a["ident"]).then_inc(small_in, 16)
                sp.wait_ge(zeros_ready, 1)
                sp.dma_start(x_dram[B:X_ROWS, :], junk[0:X_ROWS - B, :]).then_inc(zeros_stored, 16)
                sp.wait_ge(zeros_stored, 16)
                sp.wait_ge(small_in, 96)

            @block.scalar
            def _(act):
                count.append(load_weights(act, "dnn"))

            @block.vector
            def _(dve):
                nc.vector.memset(junk[:], 0.0).then_inc(zeros_ready, 1)
                dve.wait_ge(small_in, 96)
                nc.vector.tensor_copy(idx_f[:], idx_in[:]).then_inc(idx_step, 1)
                dve.wait_ge(idx_step, 1)
                nc.vector.tensor_scalar(wrap[:], idx_f[:], 0.0, float(ROWS), ALU.is_lt, ALU.mult).then_inc(idx_step, 1)
                dve.wait_ge(idx_step, 2)
                nc.vector.tensor_tensor(idx_f[:], idx_f[:], wrap[:], ALU.add).then_inc(idx_step, 1)
                dve.wait_ge(idx_step, 3)
                nc.vector.tensor_scalar(wrap[:], idx_f[:], 0.0, float(ROWS - 1), ALU.max, ALU.min) \
                  .then_inc(idx_step, 1)
                dve.wait_ge(idx_step, 4)
                nc.vector.tensor_tensor(rows[:], wrap[:], base[:].unsqueeze(1).to_broadcast([P, TILES, NS]), ALU.add) \
                  .then_inc(idx_step, 1)
                dve.wait_ge(idx_step, 5)
        with nc.Fori(0, TILES // 2) as turn:
            with nc.Block() as block:
                @block.vector
                def _(dve):
                    nc.vector.tensor_copy(rows_now[:], rows[:, bass.ds(turn * 2, 2), :]).then_inc(rows_ready, 1)
                    for j in range(2):
                        dense_j = dense[:, bass.ds(turn * 2 + j, 1), :].rearrange("p t n -> p (t n)")
                        nc.vector.tensor_tensor(x[:, j, 0:ND * E].rearrange("p (f e) -> p f e", e=E), embed[:],
                                                dense_j.unsqueeze(2).to_broadcast([P, ND, E]), ALU.mult) \
                          .then_inc(x_ready, 1)
                    for j in range(2):
                        dve.wait_ge(gathered[j], turn * 16 * NS + 16 * NS)
                        dve.wait_ge(x_ready, 2)
                        if j:
                            dve.wait_ge(lin_ready, 2)
                        nc.vector.tensor_tensor_reduce(junk[:], x[:, j, :], lin_w[:], 1.0, 0.0, ALU.mult, ALU.add,
                                                       lin_now[:, j:j + 1]).then_inc(lin_ready, 1)
                        dve.wait_ge(lin_ready, 2 * j + 1)
                        nc.vector.tensor_copy(lin_sum[:, bass.ds(turn * 2 + j, 1)], lin_now[:, j:j + 1]) \
                          .then_inc(lin_ready, 1)

                @block.gpsimd
                def _(pool):
                    pool.wait_ge(rows_ready, 1)
                    for j in range(2):
                        for n in range(NS):
                            nc.gpsimd.indirect_dma_start(
                                out=x[:, j, (ND + n) * E:(ND + n + 1) * E], out_offset=None, in_=a["table"],
                                in_offset=bass.IndirectOffsetOnAxis(ap=rows_now[:, j, n:n + 1], axis=0)) \
                              .then_inc(gathered[j], 16)

                @block.sync
                def _(sp):
                    for j in range(2):
                        sp.wait_ge(gathered[j], turn * 16 * NS + 16 * NS)
                        sp.wait_ge(x_ready, 2)
                        sp.dma_start(x_dram[bass.ds(turn * 2 * P + j * P, P), :], x[:, j, :]).then_inc(x_stored, 16)
                    sp.wait_ge(x_stored, 32)
            clear([rows_ready, x_ready, lin_ready, x_stored])
        return count[0]


def dnn_stage(nc, rows_dram, first_row, total, ident, weights, biases, weights_in, WEIGHTS, clear,
              B, K0, H1, H2, H3):
    w0, w1, w2, w3 = weights
    KC = -(-K0 // P)
    KL = K0 - (KC - 1) * P
    Q = BATCH // P
    BATCHES = B // BATCH
    with ExitStack() as ctx:
        sb = lambda name, shape, dt=F32: ctx.enter_context(nc.sbuf_tensor(name, shape, dt))
        sem = lambda name: ctx.enter_context(nc.semaphore(name))
        tag = total.name
        x = sb(f"x_rows_{tag}", [P, Q, K0])
        xT = sb(f"xT_{tag}", [P, KC, BATCH])
        h = [sb(f"h{n}_{tag}", [P, w // P, BATCH]) for n, w in enumerate((H1, H2, H3))]
        psT = ctx.enter_context(nc.psum_tensor(f"psT_{tag}", [P, 3, BATCH], F32))
        ps = ctx.enter_context(nc.psum_tensor(f"ps_{tag}", [P, 4, BATCH], F32))
        psY = ctx.enter_context(nc.psum_tensor(f"psY_{tag}", [P, Q], F32))
        x_in = [sem(f"x_in{q}_{tag}") for q in range(Q)]
        turned = sem(f"turned_{tag}")
        copied = sem(f"copied_{tag}")
        product = sem(f"product_{tag}")
        relued = sem(f"relued_{tag}")
        y_done = sem(f"y_done_{tag}")
        y_out = sem(f"y_out_{tag}")
        sems = x_in + [turned, copied, product, relued, y_done, y_out]
        TILES1, TILES2, TILES3 = H1 // P, H2 // P, H3 // P

        def load_rows(sp, n):
            for q in range(Q):
                sp.dma_start(x[:, q, :], rows_dram[bass.ds(n * BATCH + first_row + q * P, P), :]).then_inc(x_in[q], 16)

        def turn_rows(pe):
            for c in range(KC):
                k = P if c < KC - 1 else KL
                if c >= 3:
                    pe.wait_ge(copied, c - 2)
                for q in range(Q):
                    if c == 0:
                        pe.wait_ge(x_in[q], 16)
                    last = nc.tensor.transpose(psT[0:k, c % 3, q * P:(q + 1) * P], x[:, q, c * P:c * P + k], ident[:])
                last.then_inc(turned, 1)

        def copy_rows(dve):
            for c in range(KC):
                k = P if c < KC - 1 else KL
                dve.wait_ge(turned, c + 1)
                nc.vector.tensor_copy(xT[0:k, c, :], psT[0:k, c % 3, :]).then_inc(copied, 1)

        def body(n, last_turn):
            with nc.Block() as block:
                @block.sync
                def _(sp):
                    if not last_turn:
                        load_rows(sp, n + 1)

                @block.tensor
                def _(pe):
                    tile = 0
                    for layer, (src, w, kc, tiles) in enumerate(((xT, w0, KC, TILES1), (h[0], w1, TILES1, TILES2),
                                                                 (h[1], w2, TILES2, TILES3))):
                        if layer == 1 and not last_turn:
                            turn_rows(pe)
                        if layer:
                            pe.wait_ge(relued, tile)
                        for t in range(tiles):
                            if tile >= 4:
                                pe.wait_ge(relued, tile - 3)
                            for c in range(kc):
                                k = KL if layer == 0 and c == KC - 1 else P
                                last = nc.tensor.matmul(ps[:, tile % 4, :], w[0:k, c, t * P:(t + 1) * P],
                                                        src[0:k, c, :], start=(c == 0), stop=(c == kc - 1))
                            last.then_inc(product, 1)
                            tile += 1
                    pe.wait_ge(relued, tile)
                    for q in range(Q):
                        for c in range(TILES3):
                            last = nc.tensor.matmul(psY[:, q:q + 1], h[2][:, c, q * P:(q + 1) * P], w3[:, c:c + 1],
                                                    start=(c == 0), stop=(c == TILES3 - 1))
                    last.then_inc(y_done, 1)

                @block.scalar
                def _(act):
                    tile = 0
                    for layer, tiles in enumerate((TILES1, TILES2, TILES3)):
                        for t in range(tiles):
                            act.wait_ge(product, tile + 1)
                            nc.scalar.activation(h[layer][:, t, :], ps[:, tile % 4, :], ACT.Relu,
                                                 bias=biases[layer][:, t:t + 1]).then_inc(relued, 1)
                            tile += 1

                @block.vector
                def _(dve):
                    if not last_turn:
                        copy_rows(dve)
                    dve.wait_ge(y_done, 1)
                    nc.vector.tensor_copy(total[:, bass.ds(n * Q, Q)], psY[:]).then_inc(y_out, 1)
            clear(sems)

        with nc.Block() as block:
            @block.sync
            def _(sp):
                sp.wait_ge(weights_in, WEIGHTS)
                load_rows(sp, 0)

            @block.tensor
            def _(pe):
                turn_rows(pe)

            @block.vector
            def _(dve):
                copy_rows(dve)
        clear(sems)
        if BATCHES > 1:
            with nc.Fori(0, BATCHES - 1) as n:
                body(n, False)
        body(BATCHES - 1, True)


def attention_stage(nc, a, x_dram, att_dram, ident, load_weights, clear, F, K0, STEPS):
    T = PACK * F
    HF = GROUPS * F
    HC = QUADS * F
    NV = H * PACK * D
    SCALE = float(D) ** -0.5
    PAIR = 2
    PT = PAIR * F
    TT = GROUPS // PAIR
    SPLIT = 3
    HS = HF // SPLIT
    PIECES = HALVES * SPLIT
    UNITS = LAYERS * STREAMS
    with ExitStack() as ctx:
        sb = lambda name, shape, dt=F32: ctx.enter_context(nc.sbuf_tensor(name, shape, dt))
        sem = lambda name: ctx.enter_context(nc.semaphore(name))
        psum = lambda name, shape: ctx.enter_context(nc.psum_tensor(name, shape, F32))
        wq = sb("wq", [P, LAYERS, HALVES, HALVES, P])
        wr = sb("wr", [P, LAYERS, HALVES, HALVES, P])
        wv = sb("wv", [P, LAYERS, HALVES, NV])
        same_sample = sb("same_sample", [P, P])
        same_sample_v = sb("same_sample_v", [P, NV])
        is_sample = sb("is_sample", [P, PACK])
        is_quad = sb("is_quad", [P, QUADS])
        minus_diag = sb("minus_diag", [P, F])
        ones_block = sb("ones_block", [P, P])
        sum_columns = sb("sum_columns", [P, D])
        xt = [sb(f"xt{s}", [PT, TT, PACK, E]) for s in range(STREAMS)]
        shared = sb("shared", [max(PT, HS), TT * HALVES * P])
        x_perm = shared[0:PT, :].rearrange("p (t h n) -> p t h n", t=TT, h=HALVES)
        recips_wide = shared[0:HS, 0:PIECES * P].rearrange("p (c n) -> p c n", c=PIECES)
        xL = [sb(f"xL{s}", [P, HALVES, HF]) for s in range(STREAMS)]
        x_bd = sb("x_bd", [P, HALVES, GROUPS, T])
        q_bd = [sb(f"q_bd{s}", [P, HALVES, GROUPS, T]) for s in range(STREAMS)]
        q_heads = [sb(f"q_heads{s}", [P, HALVES, GROUPS, QUADS, F]) for s in range(STREAMS)]
        v_sb = [sb(f"v_sb{s}", [T, GROUPS, H, 32]) for s in range(STREAMS)]
        m = sb("m", [T, 4, H])
        m_diag = sb("m_diag", [T, 3, H, F])
        e_sb = sb("e_sb", [T, 3, H, F])
        o_sb = sb("o_sb", [P, HALVES, HF])
        recips = sb("recips", [HS, PIECES, QUADS * LANES])
        mixed = sb("mixed", [P, HALVES, HF])
        q_sb = mixed
        x_out = sb("x_out", [P, GROUPS, HALVES, F])
        psP = psum("psP", [P, HALVES, 512])
        psO = psum("psO", [P, HALVES, 512])
        psS = psum("psS", [P, 3, 512])
        psV = psum("psV", [P, 512])

        consts_in = sem("consts_in")
        consts_ready = sem("consts_ready")
        xt_in = [sem(f"xt_in{s}") for s in range(STREAMS)]
        permuted = sem("permuted")
        widened = sem("widened")
        turned = sem("rows_turned")
        x_ready = sem("x_ready_l")
        q_done = sem("q_done")
        q_copied = sem("q_copied")
        q_spread = sem("q_spread")
        x_spread = sem("x_spread")
        v_done = sem("v_done")
        v_copied = sem("v_copied")
        s_done = sem("s_done")
        max_done = sem("max_done")
        diag_done = sem("diag_done")
        shifted = sem("shifted")
        exp_done = sem("exp_done")
        mix_done = sem("mix_done")
        o_copied = sem("o_copied")
        sums_turned = sem("sums_turned")
        recip_done = sem("recip_done")
        recip_back = sem("recip_back")
        normed = sem("normed")
        res_done = sem("res_done")
        res_added = sem("res_added")
        stored = sem("stored")
        sems = xt_in + [permuted, widened, turned, x_ready, q_done, q_copied, q_spread, x_spread, v_done, v_copied, s_done, max_done,
                        diag_done, shifted, exp_done, mix_done, o_copied, sums_turned, recip_done, recip_back,
                        normed, res_done, res_added, stored]

        def load_xt(eng, s, row):
            for t in range(TT):
                for g in range(PAIR):
                    src = x_dram[bass.ds(row + PACK * (t * PAIR + g), PACK), :].rearrange("s (f e) -> f s e", e=E)
                    eng.dma_start(xt[s][g * F:(g + 1) * F, t, :, :], src).then_inc(xt_in[s], 16)
        XT = 16 * TT * PAIR

        def pe_turn(pe, s):
            for hf in range(HALVES):
                for t in range(TT):
                    last = nc.tensor.transpose(psP[:, hf, t * PT:(t + 1) * PT], x_perm[:, t, hf, :],
                                               ident[0:PT, 0:PT])
            last.then_inc(turned, 1)

        def pe_project(pe, s, w, layer, done):
            for ho in range(HALVES):
                for hi in range(HALVES):
                    last = nc.tensor.matmul(psP[:, ho, 0:HF], w[:, layer, hi, ho, :], xL[s][:, hi, :],
                                            start=(hi == 0), stop=(hi == HALVES - 1))
            last.then_inc(done, 1)

        def pe_values(pe, layer, pair):
            for j in range(PAIR):
                g = pair * PAIR + j
                for hi in range(HALVES):
                    last = nc.tensor.matmul(psV[0:T, j * 256:j * 256 + NV], x_bd[:, hi, g, :], wv[:, layer, hi, :],
                                            start=(hi == 0), stop=(hi == HALVES - 1))
            last.then_inc(v_done, 1)

        def permute(pool, s):
            for t in range(TT):
                last = nc.gpsimd.tensor_copy(
                    x_perm[:, t, :, :].rearrange("p h (q s d) -> p (h q) s d", s=LANES, d=D)[:, :, 0:PACK, :],
                    xt[s][:, t, :, :].rearrange("p s (h d) -> p h s d", d=D))
            last.then_inc(permuted, 1)

        def widen(act):
            nc.scalar.activation(recips_wide.rearrange("p c (r d) -> p c r d", d=D),
                                 recips[:].unsqueeze(3).to_broadcast([HS, PIECES, QUADS * LANES, D]), ACT.Copy) \
              .then_inc(widened, 1)

        def spread_q(dve, s):
            view = q_sb[:].rearrange("p h (g f) -> p (h g) f", f=F)
            for k in range(PACK):
                nc.vector.tensor_scalar(
                    q_bd[s][:].rearrange("p h g t -> p (h g) t")[:, :, k * F:(k + 1) * F], view,
                    is_sample[:, k:k + 1], None, ALU.mult)
            for k in range(QUADS):
                last = nc.vector.tensor_scalar(
                    q_heads[s][:].rearrange("p h g q f -> p (h g) q f")[:, :, k, :], view,
                    is_quad[:, k:k + 1], None, ALU.mult)
            last.then_inc(q_spread, 1)

        def spread_x(dve, s):
            view = xL[s][:].rearrange("p h (g f) -> p (h g) f", f=F)
            for k in range(PACK):
                last = nc.vector.tensor_scalar(
                    x_bd[:].rearrange("p h g t -> p (h g) t")[:, :, k * F:(k + 1) * F], view,
                    is_sample[:, k:k + 1], None, ALU.mult)
            last.then_inc(x_spread, 1)

        def copy_values(act, s, pair):
            nc.scalar.activation(
                v_sb[s][:, pair * PAIR:(pair + 1) * PAIR, :, 0:PACK * D],
                psV[0:T, :].rearrange("p (j n) -> p j n", j=PAIR)[:, :, 0:NV].rearrange("p j (h c) -> p j h c", h=H),
                ACT.Copy).then_inc(v_copied, 1)

        with nc.Block() as block:
            @block.sync
            def _(sp):
                for dst, name in ((same_sample, "same_sample"), (same_sample_v, "same_sample_v"),
                                  (is_sample, "is_sample"), (is_quad, "is_quad"), (minus_diag, "minus_diag"),
                                  (ones_block, "ones_block"), (sum_columns, "sum_columns")):
                    sp.dma_start(dst[:], a[name]).then_inc(consts_in, 16)
                sp.dma_start(wq[:].rearrange("p l i o n -> p (l i o n)"), a["att_wq"]).then_inc(consts_in, 16)
                sp.dma_start(wr[:].rearrange("p l i o n -> p (l i o n)"), a["att_wr"]).then_inc(consts_in, 16)
                sp.dma_start(wv[:].rearrange("p l i n -> p (l i n)"), a["att_wv"]).then_inc(consts_in, 16)
                load_xt(sp, 0, 0)

            @block.scalar
            def _(act):
                load_weights(act, "att")

            @block.vector
            def _(dve):
                nc.vector.memset(shared[:], 0.0).then_inc(consts_ready, 1)
                nc.vector.memset(xL[1][:], 0.0).then_inc(consts_ready, 1)
                nc.vector.memset(o_sb[:], 1.0).then_inc(consts_ready, 1)
                nc.vector.memset(recips[:], 1.0).then_inc(consts_ready, 1)
                dve.wait_ge(consts_in, 160)
                for w in (wq, wr):
                    flat = w[:].rearrange("p l i o n -> p (l i o) n")
                    nc.vector.tensor_tensor(flat, flat, same_sample[:].unsqueeze(1).to_broadcast(
                        [P, LAYERS * HALVES * HALVES, P]), ALU.mult).then_inc(consts_ready, 1)
                flat = wv[:].rearrange("p l i n -> p (l i) n")
                nc.vector.tensor_tensor(flat, flat, same_sample_v[:].unsqueeze(1).to_broadcast(
                    [P, LAYERS * HALVES, NV]), ALU.mult).then_inc(consts_ready, 1)
                for s in range(STREAMS):
                    nc.vector.tensor_copy(
                        v_sb[s][:, :, :, PACK * D:32].rearrange("p g h c -> p (g h) c"),
                        sum_columns[0:T, :].unsqueeze(1).to_broadcast([T, GROUPS * H, D])).then_inc(consts_ready, 1)
        clear([consts_in])
        with nc.Block() as block:
            @block.tensor
            def _(pe):
                pe.wait_ge(permuted, 1)
                pe_turn(pe, 0)
                pe.wait_ge(x_ready, 1)
                pe_project(pe, 0, wq, 0, q_done)
                pe.wait_ge(x_spread, 1)
                for pair in range(TT):
                    if pair:
                        pe.wait_ge(v_copied, pair)
                    pe_values(pe, 0, pair)

            @block.gpsimd
            def _(pool):
                pool.wait_ge(xt_in[0], XT)
                permute(pool, 0)

            @block.scalar
            def _(act):
                act.wait_ge(turned, 1)
                nc.scalar.activation(xL[0][:], psP[:, :, 0:HF], ACT.Copy).then_inc(x_ready, 1)
                act.wait_ge(q_done, 1)
                nc.scalar.activation(q_sb[:], psP[:, :, 0:HF], ACT.Copy).then_inc(q_copied, 1)
                for pair in range(TT):
                    act.wait_ge(v_done, pair + 1)
                    copy_values(act, 0, pair)

            @block.vector
            def _(dve):
                dve.wait_ge(x_ready, 1)
                spread_x(dve, 0)
                dve.wait_ge(q_copied, 1)
                spread_q(dve, 0)
        clear(sems)

        SLOTS = GROUPS + 2
        TURN_SUMS, TURN_BACK, RESIDUAL, TURN_X, QUERY, VALUES = 1, 2, 3, 4, 5, 6

        def pe_turn_sums(pe, src_count):
            for hf in range(HALVES):
                for c in range(SPLIT):
                    last = nc.tensor.transpose(psP[0:HS, hf, c * P:(c + 1) * P],
                                               o_sb[:, hf, c * HS:(c + 1) * HS], ident[:])
            last.then_inc(sums_turned, 1)

        def pe_turn_back(pe):
            for hf in range(HALVES):
                for c in range(SPLIT):
                    last = nc.tensor.transpose(psP[:, hf, c * HS:(c + 1) * HS], recips_wide[:, hf * SPLIT + c, :],
                                               ident[0:HS, 0:HS])
            last.then_inc(recip_back, 1)

        def dve_recip(dve):
            for hf in range(HALVES):
                src = psP[0:HS, hf, 0:SPLIT * P].rearrange("p (c r) -> p c r", r=32)[:, :, PACK * D:PACK * D + LANES]
                last = nc.vector.reciprocal(recips[:, hf * SPLIT:(hf + 1) * SPLIT, :].rearrange(
                    "p c (q r) -> p (c q) r", q=QUADS), src)
            last.then_inc(recip_done, 1)

        def finish_parts(f, out_layer, s, layer):
            def norm(dve):
                nc.vector.tensor_tensor(mixed[:], o_sb[:], psP[:, :, 0:HF], ALU.mult).then_inc(normed, 1)

            def add(dve):
                nc.vector.tensor_tensor(mixed[:], mixed[:], psP[:, :, 0:HF], ALU.add).then_inc(res_added, 1)

            def relu(act):
                if out_layer:
                    nc.scalar.activation(x_out[:].rearrange("p g h f -> p h g f"),
                                         mixed[:].rearrange("p h (g f) -> p h g f", f=F), ACT.Relu) \
                      .then_inc(x_ready, 1)
                else:
                    nc.scalar.activation(xL[s][:], mixed[:], ACT.Relu).then_inc(x_ready, 1)
            return norm, add, relu

        def store_out(sp, row, count):
            for q in range(QUADS):
                for k in range(PACK):
                    dst = att_dram[bass.ds(row, CHUNK), :].rearrange("(g s) n -> s g n", s=PACK)[k].rearrange(
                        "g (q d c) -> q d g c", q=QUADS, d=D)[q]
                    sp.dma_start(dst, x_out[32 * q + D * k:32 * q + D * (k + 1), :, :, :].rearrange(
                        "p g h f -> p g (h f)")).then_inc(stored, 16)
        STORE = 16 * QUADS * PACK

        def x_counts(u):
            before = sum(2 if (v + 1) % UNITS < STREAMS else 1 for v in range(u))
            first = before + 1
            return first, first + ((u + 1) % UNITS < STREAMS)

        def t_count(u):
            return sum((v + 1) % UNITS < STREAMS for v in range(u + 1))

        def p_free_x(pe, u):
            if u:
                pe.wait_ge(q_copied, u)

        with nc.Fori(0, STEPS) as turn:
            with nc.Block() as block:
                @block.sync
                def _(sp):
                    load_xt(sp, 1, turn * STEP + CHUNK)
                    load_xt(sp, 0, turn * STEP + STEP)
                    sp.wait_ge(x_ready, x_counts(0)[0])
                    store_out(sp, turn * STEP, 1)
                    sp.wait_ge(x_ready, x_counts(UNITS - 1)[0])
                    store_out(sp, turn * STEP + CHUNK, 2)
                    sp.wait_ge(stored, 2 * STORE)

                @block.tensor
                def _(pe):
                    for u in range(UNITS):
                        layer, s = u // STREAMS, u % STREAMS
                        nxt = (u + 1) % UNITS
                        nl, ns = nxt // STREAMS, nxt % STREAMS
                        fl = (u - 1) % UNITS // STREAMS
                        for slot in range(SLOTS):
                            g = slot
                            if g < GROUPS:
                                n = GROUPS * u + g
                                if g == 0 and u:
                                    pe.wait_ge(q_spread, u)
                                if n >= 3:
                                    pe.wait_ge(exp_done, n - 2)
                                for hf in range(HALVES):
                                    last = nc.tensor.matmul(psS[0:T, n % 3, hf * HC:(hf + 1) * HC],
                                                            q_bd[s][:, hf, g, :], q_heads[s][:, hf, g, :, :],
                                                            start=(hf == 0), stop=False, skip_group_check=True)
                                last.then_inc(s_done, 1)
                            if 0 <= slot - 2 < GROUPS:
                                g = slot - 2
                                n = GROUPS * u + g
                                if g == 0 and u:
                                    pe.wait_ge(v_copied, TT * u)
                                    pe.wait_ge(o_copied, u)
                                pe.wait_ge(exp_done, n + 1)
                                for h in range(H):
                                    hf, q = h // QUADS, h % QUADS
                                    last = nc.tensor.matmul(psO[32 * q:32 * q + 32, hf, g * F:(g + 1) * F],
                                                            v_sb[s][:, g, h, :], e_sb[:, n % 3, h, :],
                                                            start=True, stop=True)
                                last.then_inc(mix_done, 1)
                            if slot == TURN_SUMS:
                                if u:
                                    pe.wait_ge(o_copied, u)
                                p_free_x(pe, u)
                                pe_turn_sums(pe, u)
                            if slot == TURN_BACK:
                                pe.wait_ge(widened, u + 1)
                                pe_turn_back(pe)
                            if slot == RESIDUAL:
                                pe.wait_ge(normed, u + 1)
                                pe_project(pe, ns, wr, fl, res_done)
                            if slot == TURN_X and nxt < STREAMS:
                                pe.wait_ge(permuted, t_count(u))
                                pe.wait_ge(res_added, u + 1)
                                pe_turn(pe, ns)
                            if slot == QUERY:
                                pe.wait_ge(res_added, u + 1)
                                pe.wait_ge(x_ready, x_counts(u)[1])
                                pe_project(pe, ns, wq, nl, q_done)
                            if slot >= VALUES:
                                pair = slot - VALUES
                                if pair == 0:
                                    pe.wait_ge(x_spread, u + 1)
                                if TT * u + pair:
                                    pe.wait_ge(v_copied, TT * u + pair)
                                pe_values(pe, nl, pair)
                            if 0 <= slot - 1 < GROUPS:
                                n = GROUPS * u + slot - 1
                                pe.wait_ge(diag_done, n + 1)
                                nc.tensor.matmul(psS[0:T, n % 3, 0:H * F], ones_block[0:T, 0:T],
                                                 m_diag[:, n % 3, :, :].rearrange("p h f -> p (h f)"),
                                                 start=False, stop=True, skip_group_check=True).then_inc(shifted, 1)

                @block.vector
                def _(dve):
                    for u in range(UNITS):
                        nxt = (u + 1) % UNITS
                        nl, ns = nxt // STREAMS, nxt % STREAMS
                        norm, add, _relu = finish_parts(u, False, ns, 0)
                        for slot in range(SLOTS):
                            if slot < GROUPS:
                                n = GROUPS * u + slot
                                dve.wait_ge(s_done, n + 1)
                                if n >= 4:
                                    dve.wait_ge(diag_done, n - 3)
                                nc.vector.tensor_reduce(
                                    m[:, n % 4, :], psS[0:T, n % 3, 0:H * F].rearrange("p (h f) -> p h f", h=H),
                                    AX_X, ALU.max).then_inc(max_done, 1)
                            if slot == TURN_SUMS:
                                dve.wait_ge(sums_turned, u + 1)
                                dve_recip(dve)
                            if slot == TURN_BACK:
                                dve.wait_ge(recip_back, u + 1)
                                if u:
                                    dve.wait_ge(x_ready, x_counts(u - 1)[0])
                                norm(dve)
                            if slot == RESIDUAL:
                                dve.wait_ge(normed, u + 1)
                                dve.wait_ge(res_done, u + 1)
                                add(dve)
                            if slot == QUERY:
                                dve.wait_ge(x_ready, x_counts(u)[1])
                                dve.wait_ge(v_done, TT * u)
                                spread_x(dve, ns)
                                dve.wait_ge(q_copied, u + 1)
                                if u:
                                    dve.wait_ge(s_done, GROUPS * u)
                                spread_q(dve, ns)

                @block.gpsimd
                def _(pool):
                    for n in range(GROUPS * UNITS):
                        u, g = n // GROUPS, n % GROUPS
                        if g == RESIDUAL and (u + 1) % UNITS < STREAMS:
                            ns = (u + 1) % STREAMS
                            pool.wait_ge(xt_in[ns], XT)
                            pool.wait_ge(recip_back, u + 1)
                            permute(pool, ns)
                        pool.wait_ge(max_done, n + 1)
                        if n >= 3:
                            pool.wait_ge(shifted, n - 2)
                        nc.gpsimd.tensor_tensor(m_diag[:, n % 3, :, :],
                                                m[:, n % 4, :].unsqueeze(2).to_broadcast([T, H, F]),
                                                minus_diag[0:T, :].unsqueeze(1).to_broadcast([T, H, F]), ALU.mult) \
                          .then_inc(diag_done, 1)

                @block.scalar
                def _(act):
                    for u in range(UNITS):
                        nxt = (u + 1) % UNITS
                        nl, ns = nxt // STREAMS, nxt % STREAMS
                        fl = (u - 1) % UNITS // STREAMS
                        _norm, _add, relu = finish_parts(u, fl == LAYERS - 1, ns, 0)
                        for slot in range(SLOTS):
                            if slot == TURN_SUMS:
                                act.wait_ge(recip_done, u + 1)
                                if u:
                                    act.wait_ge(turned, t_count(u - 1))
                                widen(act)
                            if slot == RESIDUAL + 1:
                                act.wait_ge(res_added, u + 1)
                                if fl == LAYERS - 1 and u:
                                    act.wait_ge(stored, STORE)
                                relu(act)
                            if slot == TURN_X and nxt < STREAMS:
                                act.wait_ge(turned, t_count(u))
                                nc.scalar.activation(xL[ns][:], psP[:, :, 0:HF], ACT.Copy).then_inc(x_ready, 1)
                            if slot == QUERY:
                                act.wait_ge(q_done, u + 1)
                                if u:
                                    act.wait_ge(q_spread, u)
                                nc.scalar.activation(q_sb[:], psP[:, :, 0:HF], ACT.Copy).then_inc(q_copied, 1)
                            if slot > VALUES:
                                pair = slot - VALUES - 1
                                act.wait_ge(v_done, TT * u + pair + 1)
                                if pair == 0 and u:
                                    act.wait_ge(mix_done, GROUPS * u)
                                copy_values(act, ns, pair)
                            if 0 <= slot - 1 < GROUPS:
                                n = GROUPS * u + slot - 1
                                act.wait_ge(shifted, n + 1)
                                if n >= 3:
                                    act.wait_ge(mix_done, n - 2)
                                nc.scalar.activation(e_sb[:, n % 3, :, :].rearrange("p h f -> p (h f)"),
                                                     psS[0:T, n % 3, 0:H * F], ACT.Exp, scale=SCALE) \
                                  .then_inc(exp_done, 1)
                        act.wait_ge(v_done, TT * (u + 1))
                        copy_values(act, ns, TT - 1)
                        act.wait_ge(mix_done, GROUPS * (u + 1))
                        act.wait_ge(normed, u + 1)
                        nc.scalar.activation(o_sb[:], psO[:, :, 0:HF], ACT.Copy).then_inc(o_copied, 1)
            clear(sems)

        norm, add, relu = finish_parts(0, True, STREAMS - 1, LAYERS - 1)
        with nc.Block() as block:
            @block.tensor
            def _(pe):
                pe_turn_sums(pe, 0)
                pe.wait_ge(widened, 1)
                pe_turn_back(pe)
                pe.wait_ge(normed, 1)
                pe_project(pe, STREAMS - 1, wr, LAYERS - 1, res_done)

            @block.vector
            def _(dve):
                dve.wait_ge(sums_turned, 1)
                dve_recip(dve)
                dve.wait_ge(recip_back, 1)
                norm(dve)
                dve.wait_ge(normed, 1)
                dve.wait_ge(res_done, 1)
                add(dve)

            @block.scalar
            def _(act):
                act.wait_ge(recip_done, 1)
                widen(act)
                act.wait_ge(res_added, 1)
                relu(act)

            @block.sync
            def _(sp):
                sp.wait_ge(x_ready, 1)
                store_out(sp, STEPS * STEP, 1)
                sp.wait_ge(stored, STORE)


def finish_stage(nc, a, out, lin_sum, dnn_sum, att_sum, ident, TILES):
    with ExitStack() as ctx:
        sb = lambda name, shape: ctx.enter_context(nc.sbuf_tensor(name, shape, F32))
        sem = lambda name: ctx.enter_context(nc.semaphore(name))
        bias = sb("bias3", [P, 3])
        bias_sum = sb("bias_sum", [P, 1])
        y = sb("y", [P, TILES])
        yT = sb("yT", [TILES, P])
        ps = ctx.enter_context(nc.psum_tensor("ps_y", [TILES, P], F32))
        bias_in = sem("bias_in")
        step = sem("sum_step")
        y_turned = sem("y_turned")
        y_ready = sem("y_ready")
        y_stored = sem("y_stored")
        with nc.Block() as block:
            @block.sync
            def _(sp):
                for n, name in enumerate(("lin_b", "dnn_out_b", "att_out_b")):
                    sp.dma_start(bias[:, n:n + 1], a[name].partition_broadcast(P)).then_inc(bias_in, 16)
                sp.wait_ge(y_ready, 1)
                sp.dma_start(out.rearrange("(t p) -> t p", p=P), yT[:]).then_inc(y_stored, 16)
                sp.wait_ge(y_stored, 16)

            @block.vector
            def _(dve):
                dve.wait_ge(bias_in, 48)
                nc.vector.tensor_reduce(bias_sum[:], bias[:], AX_X, ALU.add).then_inc(step, 1)
                nc.vector.tensor_tensor(y[:], lin_sum[:], dnn_sum[:], ALU.add).then_inc(step, 1)
                dve.wait_ge(step, 2)
                nc.vector.tensor_tensor(y[:], y[:], att_sum[:], ALU.add).then_inc(step, 1)
                dve.wait_ge(step, 3)
                nc.vector.tensor_scalar(y[:], y[:], bias_sum[:, 0:1], None, ALU.add).then_inc(step, 1)

            @block.tensor
            def _(pe):
                pe.wait_ge(step, 4)
                nc.tensor.transpose(ps[:], y[:], ident[:]).then_inc(y_turned, 1)

            @block.scalar
            def _(act):
                act.wait_ge(y_turned, 1)
                nc.scalar.activation(yT[:], ps[:], ACT.Sigmoid).then_inc(y_ready, 1)


def lay_out(inputs):
    g = {k.replace("L0_rec_", ""): np.asarray(v) for k, v in inputs.items()}
    c = np.ascontiguousarray
    NS, ROWS, _ = g["sparse_embed"].shape
    ND = g["dense_embed"].shape[0]
    F = ND + NS
    a = {
        "dense": g["r_dense_input"], "sparse": g["r_sparse_input"],
        "table": g["sparse_embed"].reshape(NS * ROWS, E), "embed": g["dense_embed"].reshape(-1),
        "lin_w": g["lin_w"].reshape(-1), "lin_b": g["lin_b"],
        "table_base": np.arange(NS, dtype=np.float32) * ROWS,
    }
    for pre, mine in (("dnn", "dnn"), ("att_dnn", "att")):
        w0 = g[f"{pre}_w0"]
        if mine == "att":
            w0 = w0.reshape(-1, F, HALVES, QUADS, D).transpose(0, 3, 4, 2, 1).reshape(-1, F * E)
        a[mine + "_w0"], a[mine + "_w1"], a[mine + "_w2"] = w0.T, g[f"{pre}_w1"].T, g[f"{pre}_w2"].T
        a[mine + "_out_w"] = g[f"{pre}_out_w"].reshape(-1, P).T
        a[mine + "_out_b"] = g[f"{pre}_out_b"]
        for n in range(3):
            a[f"{mine}_b{n}"] = g[f"{pre}_b{n}"].reshape(-1, P).T
    for w, name in ((g["att_wq"], "att_wq"), (g["att_wr"], "att_wr")):
        t = w.reshape(LAYERS, HALVES, QUADS, D, HALVES, QUADS, D).transpose(5, 6, 0, 4, 1, 2, 3)
        t = np.broadcast_to(t[:, None, :, :, :, :, :, None, :],
                            (QUADS, LANES, D, LAYERS, HALVES, HALVES, QUADS, LANES, D))
        a[name] = t.reshape(P, -1)
    t = g["att_wv"].reshape(LAYERS, H, D, HALVES, QUADS, D).transpose(4, 5, 0, 3, 1, 2)
    t = np.broadcast_to(t[:, None, :, :, :, :, None, :], (QUADS, LANES, D, LAYERS, HALVES, H, PACK, D))
    a["att_wv"] = t.reshape(P, -1)
    a.update(constants(F))
    return {k: c(v) for k, v in a.items()}


def kernel(**inputs):
    import concourse.bacc as bacc
    from concourse.bass_utils import run_bass_kernel_spmd

    arrays = lay_out(inputs)
    nc = bacc.Bacc("TRN2", target_bir_lowering=False, num_devices=1)
    aps = {k: nc.dram_tensor(f"in_{k}", v.shape, mybir.dt.from_np(v.dtype), kind="ExternalInput").ap()
           for k, v in arrays.items()}
    B = arrays["dense"].shape[0]
    out = nc.dram_tensor("out_y", (B,), F32, kind="ExternalOutput").ap()
    build_kernel(nc, aps, out)
    r = run_bass_kernel_spmd(nc, [{f"in_{k}": v for k, v in arrays.items()}], core_ids=[0])
    return r.results[0]["out_y"]
```

```python
from contextlib import ExitStack

import numpy as np
import concourse.bass as bass
from concourse import mybir

F32 = mybir.dt.float32
F32R = mybir.dt.float32r
I32 = mybir.dt.int32
ALU = mybir.AluOpType
ACT = mybir.ActivationFunctionType
AX_X = mybir.AxisListType.X

P = 128
E = 64
H = 8
D = 8
HALVES = 2
QUADS = 4
LAYERS = 3
PACK = 3
LANES = 4
GROUPS = 8
CHUNK = GROUPS * PACK
STREAMS = 3
STEP = STREAMS * CHUNK
BATCH = 512


def constants(F):
    T = PACK * F
    p = np.arange(P)
    lane = (p // D) % LANES
    c = {}
    c["ident"] = np.eye(P)
    c["same_sample"] = (lane[:, None] == lane[None, :]) & (lane[:, None] < PACK)
    c["is_sample"] = lane[:, None] == np.arange(PACK)[None, :]
    c["minus_diag"] = -1.0 * ((p % F)[:, None] == np.arange(F)[None, :])
    ones = (p // F)[:, None] == (p // F)[None, :]
    c["ones_block"] = ones
    sample = p // F
    v = np.zeros((P, D))
    for s in range(PACK):
        v[:, s] = sample == s
    v[:, PACK] = sample == 0
    c["sum_columns"] = v
    return {k: np.ascontiguousarray(a, dtype=np.float32) for k, a in c.items()}


def build_kernel(nc, a, out):
    B = a["dense"].shape[0]
    ND, NS = a["dense"].shape[1], a["sparse"].shape[1]
    F = ND + NS
    K0 = F * E
    TILES = B // P
    STEPS = -(-B // STEP)
    x_dram = nc.dram_tensor("x_rows", ((STEPS + 1) * STEP, K0), F32, kind="Internal").ap()
    att_dram = nc.dram_tensor("att_rows", (STEPS * STEP + CHUNK, K0), F32, kind="Internal").ap()

    with ExitStack() as whole:
        sb = lambda name, shape, dt=F32: whole.enter_context(nc.sbuf_tensor(name, shape, dt))
        sem = lambda name: whole.enter_context(nc.semaphore(name))
        lin_sum = sb("lin_sum", [P, TILES])
        dnn_sum = sb("dnn_sum", [P, TILES])
        att_sum = sb("att_sum", [P, TILES])
        ident = sb("ident", [P, P])

        def clear(sems):
            with nc.Block() as block:
                @block.sync
                def _(sp):
                    for s in sems:
                        sp.sem_clear(s)

        dnn_stage(nc, sem, a, "dnn", x_dram, 0, dnn_sum, ident, clear, lin_sum)
        attention_stage(nc, sem, a, x_dram, att_dram, ident, clear, F, K0, STEPS)
        dnn_stage(nc, sem, a, "att", att_dram, CHUNK, att_sum, ident, clear, None)
        finish_stage(nc, a, out, lin_sum, dnn_sum, att_sum, ident, TILES)


def dnn_stage(nc, sem, a, pre, rows_dram, first_row, total, ident, clear, lin_sum):
    gathers = lin_sum is not None
    B, ND = a["dense"].shape
    NS = a["sparse"].shape[1]
    ROWS = a["table"].shape[0] // NS
    K0, H1 = a[pre + "_w0"].shape
    H2, H3 = a[pre + "_w1"].shape[1], a[pre + "_w2"].shape[1]
    TILES = B // P
    KC = -(-K0 // P)
    KL = K0 - (KC - 1) * P
    Q = BATCH // P
    BATCHES = B // BATCH
    TILES1, TILES2, TILES3 = H1 // P, H2 // P, H3 // P
    with ExitStack() as ctx:
        sb = lambda name, shape, dt=F32: ctx.enter_context(nc.sbuf_tensor(f"{pre}_{name}", shape, dt))
        psum = lambda name, shape: ctx.enter_context(nc.psum_tensor(f"{pre}_{name}", shape, F32))
        w0 = sb("w0_sb", [P, KC, H1])
        w1 = sb("w1_sb", [P, TILES1, H2])
        w2 = sb("w2_sb", [P, TILES2, H3])
        w3 = sb("w3_sb", [P, TILES3])
        biases = [sb(f"b{n}_sb", [P, w // P]) for n, w in enumerate((H1, H2, H3))]
        x = sb("x", [P, Q, K0])
        xT = sb("xT", [P, KC, BATCH])
        h0 = sb("h0", [P, TILES1, BATCH])
        h1 = sb("h1", [P, TILES2, BATCH])
        h = [h0, h1, h0]
        psT = psum("psT", [P, 3, BATCH])
        ps = psum("ps", [P, 4, BATCH])
        psY = psum("psY", [P, 2, Q])
        w0_in = [sem(f"{pre}_w0_in{t}") for t in range(TILES1)]
        biases_in = sem(f"{pre}_biases_in")
        rest_in = sem(f"{pre}_rest_in")
        turned = sem(f"{pre}_turned")
        copied = [sem(f"{pre}_copied{j}") for j in range(2)]
        product = sem(f"{pre}_product")
        relued = sem(f"{pre}_relued")
        y_done = sem(f"{pre}_y_done")
        y_out = sem(f"{pre}_y_out")
        sems = [turned, product, relued, y_done, y_out] + copied
        if gathers:
            rows = sb("rows", [P, TILES, NS], I32)
            rows_now = sb("rows_now", [P, Q, NS], I32)
            base = sb("table_base", [P, NS])
            dense = sb("dense_in", [P, TILES, ND])
            lin_w = sb("lin_w", [P, KC])
            lin_acc = x[:, 0, 0:BATCH]
            ones = sb("ones", [P, 1])
            embed = h1[:].rearrange("p c n -> p (c n)")[:, 0:ND * E]
            count = TILES * NS
            idx_in = h1[:].rearrange("p c n -> p (c n)")[:, 0:count].bitcast(I32).rearrange("p (t n) -> p t n", n=NS)
            idx_f, wrap = (h0[:].rearrange("p c n -> p (c n)")[:, k * count:(k + 1) * count].rearrange(
                "p (t n) -> p t n", n=NS) for k in range(2))
            small_in = sem("small_in")
            zeros_ready = sem("zeros_ready")
            zeros_stored = sem("zeros_stored")
            idx_step = sem("idx_step")
            rows_ready = sem("rows_ready")
            gathered = [sem(f"gathered{q}") for q in range(Q)]
            embed_in = sem("embed_in")
            dense_done = sem("dense_done")
            lin_step = sem("lin_step")
            lin_done = sem("lin_done")
            x_stored = sem("x_stored")
            sems += [rows_ready, embed_in, dense_done, lin_step, lin_done, x_stored]
            GATHER = 16 * NS
        else:
            x_in = [sem(f"{pre}_x_in{q}") for q in range(Q)]
            sems += x_in

        def load_weights(eng):
            full = K0 // P
            for t in range(TILES1):
                cols = slice(t * P, (t + 1) * P)
                eng.dma_start(w0[:, 0:full, cols], a[pre + "_w0"][0:full * P, cols].rearrange("(c p) n -> p c n", p=P)) \
                   .then_inc(w0_in[t], 16)
                eng.dma_start(w0[0:KL, full, cols], a[pre + "_w0"][full * P:K0, cols]).then_inc(w0_in[t], 16)
                if t == 0:
                    for n in range(3):
                        eng.dma_start(biases[n][:], a[f"{pre}_b{n}"]).then_inc(biases_in, 16)
            eng.dma_start(w1[:], a[pre + "_w1"].rearrange("(c p) n -> p c n", p=P)).then_inc(rest_in, 16)
            eng.dma_start(w2[:], a[pre + "_w2"].rearrange("(c p) n -> p c n", p=P)).then_inc(rest_in, 16)
            eng.dma_start(w3[:], a[pre + "_out_w"]).then_inc(rest_in, 16)
        BIASES = REST = 48

        def load_rows(sp, n):
            for q in range(Q):
                sp.dma_start(x[:, q, :], rows_dram[bass.ds(n * BATCH + first_row + q * P, P), :]).then_inc(x_in[q], 16)

        def gather(pool):
            pool.wait_ge(rows_ready, 1)
            for q in range(Q):
                for n in range(NS):
                    nc.gpsimd.indirect_dma_start(
                        out=x[:, q, (ND + n) * E:(ND + n + 1) * E], out_offset=None, in_=a["table"],
                        in_offset=bass.IndirectOffsetOnAxis(ap=rows_now[:, q, n:n + 1], axis=0)) \
                      .then_inc(gathered[q], 16)

        def dense_rows(dve, n):
            nc.vector.tensor_copy(rows_now[:], rows[:, bass.ds(n * Q, Q), :]).then_inc(rows_ready, 1)
            dve.wait_ge(embed_in, 16)
            for q in range(Q):
                dense_q = dense[:, bass.ds(n * Q + q, 1), :].rearrange("p t n -> p (t n)")
                nc.vector.tensor_tensor(x[:, q, 0:ND * E].rearrange("p (f e) -> p f e", e=E),
                                        embed.rearrange("p (f e) -> p f e", e=E),
                                        dense_q.unsqueeze(2).to_broadcast([P, ND, E]), ALU.mult) \
                  .then_inc(dense_done, 1)

        def linear(dve):
            dve.wait_ge(copied[0], (KC + 1) // 2)
            dve.wait_ge(copied[1], KC // 2)
            dve.wait_ge(x_stored, 16 * Q)
            nc.vector.tensor_scalar(lin_acc, xT[:, 0, :], lin_w[:, 0:1], None, ALU.mult).then_inc(lin_step, 1)
            for c in range(1, KC):
                k = P if c < KC - 1 else KL
                dve.wait_ge(lin_step, c)
                nc.vector.scalar_tensor_tensor(out=lin_acc[0:k], in0=xT[0:k, c, :], scalar=lin_w[0:k, c:c + 1],
                                               in1=lin_acc[0:k], op0=ALU.mult, op1=ALU.add).then_inc(lin_step, 1)

        def linear_sum(pe):
            pe.wait_ge(lin_step, KC)
            for q in range(Q):
                last = nc.tensor.matmul(psY[:, 1, q:q + 1], lin_acc[:, q * P:(q + 1) * P], ones[:],
                                        start=True, stop=True)
            last.then_inc(lin_done, 1)

        def linear_out(dve, n):
            dve.wait_ge(lin_done, 1)
            nc.vector.tensor_copy(lin_sum[:, bass.ds(n * Q, Q)], psY[:, 1, :]).then_inc(y_out, 1)

        def load_embed(sp):
            sp.dma_start(embed, a["embed"].partition_broadcast(P)).then_inc(embed_in, 16)

        def store_rows(sp, n):
            for q in range(Q):
                sp.wait_ge(gathered[q], n * GATHER + GATHER)
                sp.wait_ge(dense_done, q + 1)
                sp.dma_start(rows_dram[bass.ds(n * BATCH + q * P, P), :], x[:, q, :]).then_inc(x_stored, 16)
            sp.wait_ge(x_stored, 16 * Q)

        def turn_rows(pe, n):
            for c in range(KC):
                k = P if c < KC - 1 else KL
                if c >= 3:
                    pe.wait_ge(copied[(c - 3) % 2], (c - 3) // 2 + 1)
                for q in range(Q):
                    if c == 0 and gathers:
                        pe.wait_ge(gathered[q], n * GATHER + GATHER)
                        pe.wait_ge(dense_done, q + 1)
                    elif c == 0:
                        pe.wait_ge(x_in[q], 16)
                    last = nc.tensor.transpose(psT[0:k, c % 3, q * P:(q + 1) * P], x[:, q, c * P:c * P + k], ident[:])
                last.then_inc(turned, 1)

        def copy_rows(eng, j):
            for c in range(j, KC, 2):
                k = P if c < KC - 1 else KL
                eng.wait_ge(turned, c + 1)
                dst, src = xT[0:k, c, :], psT[0:k, c % 3, :]
                ins = nc.scalar.activation(dst, src, ACT.Copy) if j else nc.vector.tensor_copy(dst, src)
                ins.then_inc(copied[j], 1)

        def body(n, last_turn):
            with nc.Block() as block:
                @block.sync
                def _(sp):
                    if not last_turn and gathers:
                        load_embed(sp)
                        store_rows(sp, n + 1)
                    elif not last_turn:
                        load_rows(sp, n + 1)

                if gathers and not last_turn:
                    @block.gpsimd
                    def _(pool):
                        gather(pool)

                @block.tensor
                def _(pe):
                    tile = 0
                    for layer, (src, w, kc, tiles) in enumerate(((xT, w0, KC, TILES1), (h[0], w1, TILES1, TILES2),
                                                                 (h[1], w2, TILES2, TILES3))):
                        if layer == 1 and not last_turn:
                            turn_rows(pe, n + 1)
                        if layer == 1:
                            pe.wait_ge(rest_in, REST)
                        if layer:
                            pe.wait_ge(relued, tile)
                        for t in range(tiles):
                            if layer == 0:
                                pe.wait_ge(w0_in[t], 32)
                            if tile >= 4:
                                pe.wait_ge(relued, tile - 3)
                            for c in range(kc):
                                k = KL if layer == 0 and c == KC - 1 else P
                                last = nc.tensor.matmul(ps[:, tile % 4, :], w[0:k, c, t * P:(t + 1) * P],
                                                        src[0:k, c, :], start=(c == 0), stop=(c == kc - 1))
                            last.then_inc(product, 1)
                            tile += 1
                    if gathers and not last_turn:
                        linear_sum(pe)
                    pe.wait_ge(relued, tile)
                    if gathers and not last_turn:
                        pe.wait_ge(y_out, 1)
                    for q in range(Q):
                        for c in range(TILES3):
                            last = nc.tensor.matmul(psY[:, 0, q:q + 1], h[2][:, c, q * P:(q + 1) * P], w3[:, c:c + 1],
                                                    start=(c == 0), stop=(c == TILES3 - 1))
                    last.then_inc(y_done, 1)

                @block.scalar
                def _(act):
                    act.wait_ge(biases_in, BIASES)
                    tile = 0
                    for layer, tiles in enumerate((TILES1, TILES2, TILES3)):
                        if layer == 1 and not last_turn:
                            copy_rows(act, 1)
                        if layer == 1 and gathers and not last_turn:
                            act.wait_ge(dense_done, Q)
                        for t in range(tiles):
                            act.wait_ge(product, tile + 1)
                            if layer == 2 and t == 0:
                                act.wait_ge(product, TILES1 + TILES2)
                            nc.scalar.activation(h[layer][:, t, :], ps[:, tile % 4, :], ACT.Relu,
                                                 bias=biases[layer][:, t:t + 1]).then_inc(relued, 1)
                            tile += 1

                @block.vector
                def _(dve):
                    if not last_turn and gathers:
                        dense_rows(dve, n + 1)
                    if not last_turn:
                        copy_rows(dve, 0)
                    if not last_turn and gathers:
                        linear(dve)
                        linear_out(dve, n + 1)
                    dve.wait_ge(y_done, 1)
                    nc.vector.tensor_copy(total[:, bass.ds(n * Q, Q)], psY[:, 0, :]).then_inc(y_out, 1)
            clear(sems)

        if gathers:
            with nc.Block() as block:
                @block.sync
                def _(sp):
                    sp.dma_start(idx_in, a["sparse"].rearrange("(t p) n -> p t n", p=P)).then_inc(small_in, 16)
                    sp.dma_start(dense[:], a["dense"].rearrange("(t p) n -> p t n", p=P)).then_inc(small_in, 16)
                    sp.dma_start(base[:], a["table_base"].partition_broadcast(P)).then_inc(small_in, 16)
                    sp.dma_start(lin_w[:], a["lin_w"]).then_inc(small_in, 16)
                    sp.dma_start(ident[:], a["ident"]).then_inc(small_in, 16)
                    sp.wait_ge(zeros_ready, 1)
                    pieces = range(B, rows_dram.shape[0], P)
                    for row in pieces:
                        count = min(P, rows_dram.shape[0] - row)
                        sp.dma_start(rows_dram[row:row + count, :], x[0:count, 0, :]).then_inc(zeros_stored, 16)
                    sp.wait_ge(zeros_stored, 16 * len(pieces))

                @block.scalar
                def _(act):
                    load_weights(act)

                @block.vector
                def _(dve):
                    nc.vector.memset(x[:, 0, :], 0.0).then_inc(zeros_ready, 1)
                    nc.vector.memset(ones[:], 1.0).then_inc(idx_step, 1)
                    dve.wait_ge(small_in, 80)
                    nc.vector.tensor_copy(idx_f, idx_in).then_inc(idx_step, 1)
                    dve.wait_ge(idx_step, 2)
                    nc.vector.tensor_scalar(wrap, idx_f, 0.0, float(ROWS), ALU.is_lt, ALU.mult).then_inc(idx_step, 1)
                    dve.wait_ge(idx_step, 3)
                    nc.vector.tensor_tensor(idx_f, idx_f, wrap, ALU.add).then_inc(idx_step, 1)
                    dve.wait_ge(idx_step, 4)
                    nc.vector.tensor_scalar(wrap, idx_f, 0.0, float(ROWS - 1), ALU.max, ALU.min) \
                      .then_inc(idx_step, 1)
                    dve.wait_ge(idx_step, 5)
                    nc.vector.tensor_tensor(rows[:], wrap, base[:].unsqueeze(1).to_broadcast([P, TILES, NS]),
                                            ALU.add).then_inc(idx_step, 1)
                    dve.wait_ge(idx_step, 6)
            with nc.Block() as block:
                @block.gpsimd
                def _(pool):
                    gather(pool)

                @block.sync
                def _(sp):
                    load_embed(sp)
                    store_rows(sp, 0)

                @block.tensor
                def _(pe):
                    turn_rows(pe, 0)
                    linear_sum(pe)

                @block.scalar
                def _(act):
                    copy_rows(act, 1)

                @block.vector
                def _(dve):
                    dense_rows(dve, 0)
                    copy_rows(dve, 0)
                    linear(dve)
                    linear_out(dve, 0)
        else:
            with nc.Block() as block:
                @block.sync
                def _(sp):
                    load_rows(sp, 0)

                @block.scalar
                def _(act):
                    load_weights(act)
                    copy_rows(act, 1)

                @block.tensor
                def _(pe):
                    turn_rows(pe, 0)

                @block.vector
                def _(dve):
                    copy_rows(dve, 0)
        clear(sems)
        if BATCHES > 1:
            with nc.Fori(0, BATCHES - 1) as n:
                body(n, False)
        body(BATCHES - 1, True)


def attention_stage(nc, sem, a, x_dram, att_dram, ident, clear, F, K0, STEPS):
    T = PACK * F
    HF = GROUPS * F
    HC = QUADS * F
    SCALE = float(D) ** -0.5
    PAIR = 2
    PT = PAIR * F
    TT = GROUPS // PAIR
    SPLIT = 3
    HS = HF // SPLIT
    PIECES = HALVES * SPLIT
    UNITS = LAYERS * STREAMS
    WT = LAYERS * HALVES * HALVES
    HI, LO = 0, 1
    PRODUCTS = ((HI, HI), (HI, LO), (LO, HI))
    with ExitStack() as ctx:
        sb = lambda name, shape, dt=F32: ctx.enter_context(nc.sbuf_tensor(name, shape, dt))
        psum = lambda name, shape: ctx.enter_context(nc.psum_tensor(name, shape, F32))
        wq, wv, wr = (sb(n, [P, 2, LAYERS, HALVES, HALVES, P], F32R) for n in ("wq", "wv", "wr"))
        is_sample = sb("is_sample", [P, PACK])
        minus_diag = sb("minus_diag", [P, F])
        ones_block = sb("ones_block", [P, P])
        v_sb = sb("v_sb", [T, GROUPS, H, 32])
        o_sb = sb("o_sb", [P, HALVES, HF])
        xt = [sb(f"xt{s}", [PT, TT, PACK, E]) for s in range(STREAMS)]
        xL = [sb(f"xL{s}", [P, 2, HALVES, HF], F32R) for s in range(STREAMS)]
        q_bd = [sb(f"q_bd{s}", [P, HALVES, GROUPS, T]) for s in range(STREAMS)]
        q_heads = [sb(f"q_heads{s}", [P, HALVES, GROUPS, QUADS, F]) for s in range(STREAMS)]
        x_perm = sb("x_perm", [PT, TT, HALVES, P])
        recips_wide = sb("recips_wide", [HS, PIECES, P])
        psP = psum("psP", [P, HALVES, 512])
        psO = psum("psO", [P, HALVES, 512])
        psS = psum("psS", [P, 3, 512])
        psV = psum("psV", [P, 512])

        consts_in = sem("consts_in")
        consts_step = sem("consts_step")
        consts_ready = sem("consts_ready")

        with ExitStack() as early:
            raw = {n: early.enter_context(nc.sbuf_tensor(n + "_raw", [P, WT, P], F32)) for n in ("wq", "wv", "wr")}
            same_sample = early.enter_context(nc.sbuf_tensor("same_sample", [P, P], F32))
            sum_columns = early.enter_context(nc.sbuf_tensor("sum_columns", [P, D], F32))
            with nc.Block() as block:
                @block.sync
                def _(sp):
                    for dst, name in ((same_sample, "same_sample"), (ones_block, "ones_block"),
                                      (sum_columns, "sum_columns"), (is_sample, "is_sample"),
                                      (minus_diag, "minus_diag")):
                        sp.dma_start(dst[:], a[name]).then_inc(consts_in, 16)
                    for n in ("wq", "wv", "wr"):
                        sp.dma_start(raw[n][:].rearrange("p t n -> p (t n)"), a["att_" + n]).then_inc(consts_in, 16)

                @block.gpsimd
                def _(pool):
                    nc.gpsimd.memset(x_perm[:], 0.0).then_inc(consts_ready, 1)
                    nc.gpsimd.memset(xL[STREAMS - 1][:].bitcast(F32), 0.0).then_inc(consts_ready, 1)
                    for s in range(STREAMS):
                        nc.gpsimd.memset(q_heads[s][:], 0.0).then_inc(consts_ready, 1)

                @block.vector
                def _(dve):
                    nc.vector.memset(o_sb[:], 1.0).then_inc(consts_ready, 1)
                    nc.vector.memset(psO[:], 1.0).then_inc(consts_ready, 1)
                    dve.wait_ge(consts_in, 128)
                    for k, (n, w) in enumerate((("wq", wq), ("wv", wv), ("wr", wr))):
                        w_hi, w_lo = (w[:, part].rearrange("p l i o n -> p (l i o) n") for part in (HI, LO))
                        nc.vector.tensor_tensor(raw[n][:], raw[n][:], same_sample[:].unsqueeze(1).to_broadcast(
                            [P, WT, P]), ALU.mult).then_inc(consts_step, 1)
                        dve.wait_ge(consts_step, 2 * k + 1)
                        nc.vector.tensor_copy(w_hi, raw[n][:]).then_inc(consts_step, 1)
                        dve.wait_ge(consts_step, 2 * k + 2)
                        nc.vector.tensor_tensor(w_lo, raw[n][:], w_hi.bitcast(F32), ALU.subtract) \
                          .then_inc(consts_ready, 1)
                    nc.vector.tensor_copy(
                        v_sb[:, :, :, PACK * D:32].rearrange("p g h c -> p (g h) c"),
                        sum_columns[0:T, :].unsqueeze(1).to_broadcast([T, GROUPS * H, D])).then_inc(consts_ready, 1)
        m = sb("m", [T, 4, H])
        m_diag = sb("m_diag", [T, 3, H, F])
        e_sb = sb("e_sb", [T, 3, H, F])
        recips = sb("recips", [HS, PIECES, QUADS * LANES])
        mixed = sb("mixed", [P, HALVES, HF])
        q_sb = sb("q_sb", [P, HALVES, HF])
        v_bd = [sb(f"v_bd{s}", [P, HALVES, GROUPS, T]) for s in range(STREAMS)]
        x_out = sb("x_out", [P, GROUPS, HALVES, F])

        xt_in = [sem(f"xt_in{s}") for s in range(STREAMS)]
        permuted = sem("permuted")
        widened = sem("widened")
        turned = sem("rows_turned")
        taken_hi = sem("taken_hi")
        taken_lo = sem("taken_lo")
        hi_ready = sem("hi_ready")
        lo_ready = sem("lo_ready")
        q_done = sem("q_done")
        q_copied = sem("q_copied")
        q_spread = sem("q_spread")
        vals_done = sem("vals_done")
        vals_spread = sem("vals_spread")
        v_done = sem("v_done")
        v_copied = sem("v_copied")
        s_done = sem("s_done")
        max_done = sem("max_done")
        diag_ready = sem("diag_ready")
        shifted = sem("shifted")
        exp_done = sem("exp_done")
        mix_done = sem("mix_done")
        o_copied = sem("o_copied")
        sums_turned = sem("sums_turned")
        recip_done = sem("recip_done")
        recip_back = sem("recip_back")
        normed = sem("normed")
        res_done = sem("res_done")
        res_added = sem("res_added")
        stored = sem("stored")
        sems = xt_in + [taken_hi, taken_lo, permuted, widened, turned, hi_ready, lo_ready, q_done, q_copied, q_spread, vals_done,
                        vals_spread, v_done, v_copied, s_done, max_done, diag_ready, shifted,
                        exp_done, mix_done, o_copied, sums_turned, recip_done, recip_back, normed, res_done,
                        res_added, stored]

        def load_xt(eng, s, row):
            for t in range(TT):
                for g in range(PAIR):
                    src = x_dram[bass.ds(row + PACK * (t * PAIR + g), PACK), :].rearrange("s (f e) -> f s e", e=E)
                    eng.dma_start(xt[s][g * F:(g + 1) * F, t, :, :], src).then_inc(xt_in[s], 16)
        XT = 16 * TT * PAIR

        def store_out(sp, row):
            for q in range(QUADS):
                for k in range(PACK):
                    dst = att_dram[bass.ds(row, CHUNK), :].rearrange("(g s) n -> s g n", s=PACK)[k].rearrange(
                        "g (q d c) -> q d g c", q=QUADS, d=D)[q]
                    sp.dma_start(dst, x_out[32 * q + D * k:32 * q + D * (k + 1), :, :, :].rearrange(
                        "p g h f -> p g (h f)")).then_inc(stored, 16)
        STORE = 16 * QUADS * PACK

        def pe_turn(pe):
            for hf in range(HALVES):
                for t in range(TT):
                    last = nc.tensor.transpose(psP[:, hf, t * PT:(t + 1) * PT], x_perm[:, t, hf, :],
                                               ident[0:PT, 0:PT])
            last.then_inc(turned, 1)

        def pe_project(pe, s, w, layer, done, halves=range(HALVES)):
            for ho in halves:
                steps = [(hi, wp, xp) for wp, xp in PRODUCTS for hi in range(HALVES)]
                for n, (hi, wp, xp) in enumerate(steps):
                    last = nc.tensor.matmul(psP[:, ho, 0:HF], w[:, wp, layer, hi, ho, :], xL[s][:, xp, hi, :],
                                            start=(n == 0), stop=(n == len(steps) - 1))
            if ho == HALVES - 1:
                last.then_inc(done, 1)

        def pe_values(pe, s, pair):
            for j in range(PAIR):
                for hf in range(HALVES):
                    last = nc.tensor.transpose(psV[0:T, (j * HALVES + hf) * P:(j * HALVES + hf + 1) * P],
                                               v_bd[s][:, hf, pair * PAIR + j, :], ident[:])
            last.then_inc(v_done, 1)

        def pe_turn_sums(pe):
            for hf in range(HALVES):
                for c in range(SPLIT):
                    last = nc.tensor.transpose(psP[0:HS, hf, c * P:(c + 1) * P],
                                               o_sb[:, hf, c * HS:(c + 1) * HS], ident[:])
            last.then_inc(sums_turned, 1)

        def pe_turn_back(pe):
            for hf in range(HALVES):
                for c in range(SPLIT):
                    last = nc.tensor.transpose(psP[:, hf, c * HS:(c + 1) * HS], recips_wide[:, hf * SPLIT + c, :],
                                               ident[0:HS, 0:HS])
            last.then_inc(recip_back, 1)

        def dve_recip(dve):
            for hf in range(HALVES):
                src = psP[0:HS, hf, 0:SPLIT * P].rearrange("p (c r) -> p c r", r=32)[:, :, PACK * D:PACK * D + LANES]
                last = nc.vector.reciprocal(recips[:, hf * SPLIT:(hf + 1) * SPLIT, :].rearrange(
                    "p c (q r) -> p (c q) r", q=QUADS), src)
            last.then_inc(recip_done, 1)

        def act_widen(act):
            nc.scalar.activation(recips_wide.rearrange("p c (r d) -> p c r d", d=D),
                                 recips[:].unsqueeze(3).to_broadcast([HS, PIECES, QUADS * LANES, D]), ACT.Copy) \
              .then_inc(widened, 1)

        def dve_norm(dve):
            nc.vector.tensor_tensor(mixed[:], o_sb[:], psP[:, :, 0:HF], ALU.mult).then_inc(normed, 1)

        def dve_add(dve):
            nc.vector.tensor_tensor(mixed[:], mixed[:], psP[:, :, 0:HF], ALU.add).then_inc(res_added, 1)

        def dve_copy_mixed(dve):
            nc.vector.tensor_copy(o_sb[:], psO[:, :, 0:HF]).then_inc(o_copied, 1)

        def act_relu(act, s, is_out):
            if is_out:
                nc.scalar.activation(x_out[:].rearrange("p g h f -> p h g f"),
                                     mixed[:].rearrange("p h (g f) -> p h g f", f=F), ACT.Relu) \
                  .then_inc(hi_ready, 1)
            else:
                nc.scalar.activation(xL[s][:, HI], mixed[:], ACT.Relu).then_inc(hi_ready, 1)

        def dve_low(dve, s):
            nc.vector.scalar_tensor_tensor(out=xL[s][:, LO], in0=mixed[:], scalar=0.0,
                                           in1=xL[s][:, HI].bitcast(F32), op0=ALU.max, op1=ALU.subtract) \
              .then_inc(lo_ready, 1)

        def act_take(act, s):
            nc.scalar.activation(xL[s][:, HI], psP[:, :, 0:HF], ACT.Copy).then_inc(taken_hi, 1)

        def dve_take_low(dve, s):
            nc.vector.tensor_tensor(xL[s][:, LO], psP[:, :, 0:HF], xL[s][:, HI].bitcast(F32), ALU.subtract) \
              .then_inc(taken_lo, 1)

        def permute(pool, s, t):
            nc.gpsimd.tensor_copy(
                x_perm[:, t, :, :].rearrange("p h (q s d) -> p (h q) s d", s=LANES, d=D)[:, :, 0:PACK, :],
                xt[s][:, t, :, :].rearrange("p s (h d) -> p h s d", d=D)).then_inc(permuted, 1)

        def act_copy_q(act):
            nc.scalar.activation(q_sb[:], psP[:, :, 0:HF], ACT.Copy).then_inc(q_copied, 1)

        def by_group(t):
            return t[:].rearrange("p h (g f) -> p (h g) f", f=F)

        def q_block(eng, s, k):
            return nc.vector.tensor_scalar(q_bd[s][:].rearrange("p h g t -> p (h g) t")[:, :, k * F:(k + 1) * F],
                                           by_group(q_sb), is_sample[:, k:k + 1], None, ALU.mult)

        def q_head(engine, s, k):
            rows = slice(32 * k, 32 * k + 32)
            dst = q_heads[s][rows, :, :, k, :].rearrange("p h g f -> p (h g) f")
            src = q_sb[rows].rearrange("p h (g f) -> p (h g) f", f=F)
            if engine is nc.scalar:
                return nc.scalar.activation(dst, src, ACT.Copy)
            return engine.tensor_copy(dst, src)

        def act_value_block(act, s, k):
            return nc.scalar.activation(v_bd[s][:, :, :, k * F:(k + 1) * F],
                                        psP[:, :, 0:HF].rearrange("p h (g f) -> p h g f", f=F), ACT.Copy,
                                        scale=is_sample[:, k:k + 1])

        def act_copy_values(act, pair):
            nc.scalar.activation(
                v_sb[:, pair * PAIR:(pair + 1) * PAIR, :, 0:PACK * D].rearrange("p g h c -> p (g h) c"),
                psV[0:T, :].rearrange("p (j c) -> p j c", c=32)[:, :, 0:PACK * D],
                ACT.Copy).then_inc(v_copied, 1)

        clear([consts_in])
        with nc.Block() as block:
            @block.sync
            def _(sp):
                for s in range(STREAMS):
                    load_xt(sp, s, s * CHUNK)
                sp.wait_ge(xt_in[STREAMS - 1], XT)

            @block.gpsimd
            def _(pool):
                pool.wait_ge(xt_in[0], XT)
                for t in range(TT):
                    permute(pool, 0, t)
                pool.wait_ge(xt_in[1], XT)
                pool.wait_ge(turned, 1)
                for t in range(TT):
                    permute(pool, 1, t)

            @block.tensor
            def _(pe):
                pe.wait_ge(permuted, TT)
                pe_turn(pe)
                pe.wait_ge(taken_lo, 1)
                pe_project(pe, 0, wq, 0, q_done)
                pe.wait_ge(q_copied, 1)
                pe_project(pe, 0, wv, 0, vals_done)
                pe.wait_ge(permuted, 2 * TT)
                pe.wait_ge(vals_spread, 1)
                pe_turn(pe)

            @block.scalar
            def _(act):
                act.wait_ge(turned, 1)
                act_take(act, 0)
                act.wait_ge(q_done, 1)
                act_copy_q(act)
                act.wait_ge(q_copied, 1)
                q_head(nc.scalar, 0, 0)
                q_head(nc.scalar, 0, 1).then_inc(q_spread, 1)
                act.wait_ge(vals_done, 1)
                for k in range(PACK):
                    last = act_value_block(act, 0, k)
                last.then_inc(vals_spread, 1)
                act.wait_ge(turned, 2)
                act_take(act, 1)

            @block.vector
            def _(dve):
                dve.wait_ge(taken_hi, 1)
                dve_take_low(dve, 0)
                dve.wait_ge(q_copied, 1)
                for k in range(PACK):
                    q_block(dve, 0, k)
                q_head(nc.vector, 0, 2)
                q_head(nc.vector, 0, 3).then_inc(q_spread, 1)
                dve.wait_ge(taken_hi, 2)
                dve_take_low(dve, 1)
        clear(sems)

        VALUES, TURN_SUMS, QUERY, TURN_BACK, RESIDUAL, TURN_X = 0, 2, 3, 4, 5, 6
        PAIR_AT = (1, 2, 4, 7)
        SLOTS = GROUPS * UNITS
        TAIL = 2
        stream = lambda u: u % UNITS % STREAMS
        layer = lambda u: u % UNITS // STREAMS
        is_out = [layer(u - 1) == LAYERS - 1 for u in range(UNITS)]
        assert is_out == [layer(u + 2) == 0 for u in range(UNITS)]
        outs = lambda u: sum(is_out[:u + 1])
        res_at = lambda u: (RESIDUAL,) if is_out[u] else (RESIDUAL, RESIDUAL + 1)
        lows = lambda u: u + 1 - outs(u)

        with nc.Fori(0, STEPS) as turn:
            with nc.Block() as block:
                @block.sync
                def _(sp):
                    for s in range(STREAMS - 1):
                        load_xt(sp, s, turn * STEP + STEP + s * CHUNK)
                    for k, u in enumerate(u for u in range(UNITS) if is_out[u]):
                        if u == 0:
                            sp.wait_ge(permuted, TT)
                            load_xt(sp, STREAMS - 1, turn * STEP + STEP + (STREAMS - 1) * CHUNK)
                        sp.wait_ge(hi_ready, u + 1)
                        store_out(sp, turn * STEP + k * CHUNK)
                    sp.wait_ge(stored, outs(UNITS - 1) * STORE)
                    sp.wait_ge(xt_in[STREAMS - 1], XT)

                @block.tensor
                def _(pe):
                    for n in range(SLOTS + TAIL):
                        u, g = n // GROUPS, n % GROUPS
                        s = stream(u)
                        if n < SLOTS:
                            if g == 0 and u:
                                pe.wait_ge(q_spread, 2 * u)
                            if n >= 3:
                                pe.wait_ge(exp_done, n - 2)
                            for hf in range(HALVES):
                                last = nc.tensor.matmul(psS[0:T, n % 3, hf * HC:(hf + 1) * HC],
                                                        q_bd[s][:, hf, g, :], q_heads[s][:, hf, g, :, :],
                                                        start=(hf == 0), stop=False, skip_group_check=True)
                            last.then_inc(s_done, 1)
                        if n < SLOTS:
                            if g == VALUES:
                                if u and is_out[u - 1]:
                                    pe.wait_ge(taken_lo, outs(u - 1))
                                elif u:
                                    pe.wait_ge(lo_ready, lows(u - 1))
                                pe_project(pe, stream(u + 1), wv, layer(u + 1), vals_done)
                            if g in PAIR_AT:
                                pair = PAIR_AT.index(g)
                                if pair == 0 and u:
                                    pe.wait_ge(vals_spread, u)
                                if TT * u + pair:
                                    pe.wait_ge(v_copied, TT * u + pair)
                                pe_values(pe, s, pair)
                            if g == TURN_SUMS:
                                if u:
                                    pe.wait_ge(o_copied, u)
                                pe.wait_ge(vals_spread, u + 1)
                                pe_turn_sums(pe)
                            if g == QUERY:
                                pe.wait_ge(recip_done, u + 1)
                                pe_project(pe, stream(u + 1), wq, layer(u + 1), q_done)
                            if g == TURN_BACK:
                                pe.wait_ge(q_copied, u + 1)
                                pe.wait_ge(widened, u + 1)
                                pe_turn_back(pe)
                            if g == RESIDUAL:
                                pe.wait_ge(normed, u + 1)
                            if g in res_at(u):
                                pe_project(pe, stream(u - 1), wr, layer(u - 1), res_done,
                                           range(HALVES) if is_out[u] else (res_at(u).index(g),))
                            if g == TURN_X and is_out[u]:
                                pe.wait_ge(permuted, TT * outs(u))
                                pe.wait_ge(res_added, u + 1)
                                pe_turn(pe)
                        if n >= 2:
                            mu, mg = (n - 2) // GROUPS, (n - 2) % GROUPS
                            if mg == 0 and mu:
                                pe.wait_ge(o_copied, mu)
                            if mg % PAIR == 0:
                                pe.wait_ge(v_copied, TT * mu + mg // PAIR + 1)
                            pe.wait_ge(exp_done, n - 1)
                            for h in range(H):
                                hf, q = h // QUADS, h % QUADS
                                last = nc.tensor.matmul(
                                    psO[32 * q:32 * q + PACK * (D + 1), hf, mg * F:(mg + 1) * F],
                                    v_sb[:, mg, h, 0:PACK * (D + 1)], e_sb[:, (n - 2) % 3, h, :],
                                    start=True, stop=True)
                            last.then_inc(mix_done, 1)
                        if 1 <= n <= SLOTS:
                            pe.wait_ge(diag_ready, n)
                            nc.tensor.matmul(psS[0:T, (n - 1) % 3, 0:H * F], ones_block[0:T, 0:T],
                                             m_diag[:, (n - 1) % 3].rearrange("p h f -> p (h f)"),
                                             start=False, stop=True, skip_group_check=True).then_inc(shifted, 1)

                @block.vector
                def _(dve):
                    for n in range(SLOTS):
                        u, g = n // GROUPS, n % GROUPS
                        dve.wait_ge(s_done, n + 1)
                        if n >= 4:
                            dve.wait_ge(diag_ready, n - 3)
                        nc.vector.tensor_reduce(
                            m[:, n % 4, :], psS[0:T, n % 3, 0:H * F].rearrange("p (h f) -> p h f", h=H),
                            AX_X, ALU.max).then_inc(max_done, 1)
                        if g == TAIL - 1 and u:
                            dve.wait_ge(mix_done, GROUPS * u)
                            dve.wait_ge(normed, u)
                            dve_copy_mixed(dve)
                        if g == TURN_SUMS:
                            dve.wait_ge(sums_turned, u + 1)
                            if u:
                                dve.wait_ge(widened, u)
                            dve_recip(dve)
                        if g == TURN_BACK:
                            dve.wait_ge(recip_back, u + 1)
                            if u:
                                dve.wait_ge(hi_ready, u)
                            dve_norm(dve)
                            dve.wait_ge(q_copied, u + 1)
                            q_block(dve, stream(u + 1), 0)
                        if g == TURN_BACK:
                            q_head(nc.vector, stream(u + 1), 2)
                        if g == RESIDUAL:
                            q_block(dve, stream(u + 1), 1)
                            q_block(dve, stream(u + 1), 2)
                            q_head(nc.vector, stream(u + 1), 3).then_inc(q_spread, 1)
                        if g == res_at(u)[-1]:
                            dve.wait_ge(normed, u + 1)
                            dve.wait_ge(res_done, u + 1)
                            dve_add(dve)
                        if g == TURN_X + 1:
                            if not is_out[u]:
                                dve.wait_ge(hi_ready, u + 1)
                                dve_low(dve, stream(u - 1))
                            if is_out[u]:
                                dve.wait_ge(taken_hi, outs(u))
                                dve_take_low(dve, stream(u + 2))
                    dve.wait_ge(mix_done, SLOTS)
                    dve.wait_ge(normed, UNITS)
                    dve_copy_mixed(dve)

                @block.gpsimd
                def _(pool):
                    for n in range(SLOTS):
                        u, g = n // GROUPS, n % GROUPS
                        pool.wait_ge(max_done, n + 1)
                        if n >= 3:
                            pool.wait_ge(shifted, n - 2)
                        nc.gpsimd.tensor_tensor(m_diag[:, n % 3],
                                                m[:, n % 4, :].unsqueeze(2).to_broadcast([T, H, F]),
                                                minus_diag[0:T, :].unsqueeze(1).to_broadcast([T, H, F]), ALU.mult) \
                          .then_inc(diag_ready, 1)
                        if is_out[u] and 1 <= g <= TT:
                            if g == 1:
                                if stream(u + 2) < STREAMS - 1:
                                    pool.wait_ge(xt_in[stream(u + 2)], XT)
                                if u:
                                    pool.wait_ge(turned, outs(u - 1))
                            permute(pool, stream(u + 2), g - 1)

                @block.scalar
                def _(act):
                    for n in range(SLOTS + TAIL):
                        u, g = n // GROUPS, n % GROUPS
                        if n < SLOTS and g in PAIR_AT:
                            pair = PAIR_AT.index(g)
                            act.wait_ge(v_done, TT * u + pair + 1)
                            if u:
                                act.wait_ge(mix_done, GROUPS * (u - 1) + PAIR * (pair + 1))
                            act_copy_values(act, pair)
                        if 1 <= n <= SLOTS:
                            act.wait_ge(shifted, n)
                            if n >= 4:
                                act.wait_ge(mix_done, n - 3)
                            nc.scalar.activation(e_sb[:, (n - 1) % 3].rearrange("p h f -> p (h f)"),
                                                 psS[0:T, (n - 1) % 3, 0:H * F], ACT.Exp, scale=SCALE) \
                              .then_inc(exp_done, 1)
                        if n >= SLOTS:
                            continue
                        ns = stream(u + 1)
                        if g == VALUES:
                            act.wait_ge(vals_done, u + 1)
                            act_value_block(act, ns, 0)
                            act_value_block(act, ns, 1)
                        if g == VALUES + 1:
                            act_value_block(act, ns, 2).then_inc(vals_spread, 1)
                        if g == TURN_SUMS:
                            act.wait_ge(recip_done, u + 1)
                            if u:
                                act.wait_ge(recip_back, u)
                            act_widen(act)
                        if g == QUERY:
                            act.wait_ge(q_done, u + 1)
                            if u:
                                act.wait_ge(q_spread, 2 * u)
                            act_copy_q(act)
                        if g == QUERY + 1:
                            act.wait_ge(q_copied, u + 1)
                            q_head(nc.scalar, ns, 0)
                            q_head(nc.scalar, ns, 1).then_inc(q_spread, 1)
                        if g == res_at(u)[-1]:
                            act.wait_ge(res_added, u + 1)
                            if is_out[u] and u:
                                act.wait_ge(stored, outs(u - 1) * STORE)
                            act_relu(act, stream(u - 1), is_out[u])
                        if g == TURN_X:
                            if is_out[u]:
                                act.wait_ge(turned, outs(u))
                                act_take(act, stream(u + 2))
            clear(sems)

        with nc.Block() as block:
            @block.tensor
            def _(pe):
                pe_turn_sums(pe)
                pe.wait_ge(widened, 1)
                pe_turn_back(pe)
                pe.wait_ge(normed, 1)
                pe_project(pe, STREAMS - 1, wr, LAYERS - 1, res_done)

            @block.vector
            def _(dve):
                dve.wait_ge(sums_turned, 1)
                dve_recip(dve)
                dve.wait_ge(recip_back, 1)
                dve_norm(dve)
                dve.wait_ge(normed, 1)
                dve.wait_ge(res_done, 1)
                dve_add(dve)

            @block.scalar
            def _(act):
                act.wait_ge(recip_done, 1)
                act_widen(act)
                act.wait_ge(res_added, 1)
                act_relu(act, STREAMS - 1, True)

            @block.sync
            def _(sp):
                sp.wait_ge(hi_ready, 1)
                store_out(sp, STEPS * STEP)
                sp.wait_ge(stored, STORE)


def finish_stage(nc, a, out, lin_sum, dnn_sum, att_sum, ident, TILES):
    with ExitStack() as ctx:
        sb = lambda name, shape: ctx.enter_context(nc.sbuf_tensor(name, shape, F32))
        sem = lambda name: ctx.enter_context(nc.semaphore(name))
        bias = sb("bias3", [P, 3])
        bias_sum = sb("bias_sum", [P, 1])
        y = sb("y", [P, TILES])
        yT = sb("yT", [TILES, P])
        ps = ctx.enter_context(nc.psum_tensor("ps_y", [TILES, P], F32))
        bias_in = sem("bias_in")
        step = sem("sum_step")
        y_turned = sem("y_turned")
        y_ready = sem("y_ready")
        y_stored = sem("y_stored")
        with nc.Block() as block:
            @block.sync
            def _(sp):
                for n, name in enumerate(("lin_b", "dnn_out_b", "att_out_b")):
                    sp.dma_start(bias[:, n:n + 1], a[name].partition_broadcast(P)).then_inc(bias_in, 16)
                sp.wait_ge(y_ready, 1)
                sp.dma_start(out.rearrange("(t p) -> t p", p=P), yT[:]).then_inc(y_stored, 16)
                sp.wait_ge(y_stored, 16)

            @block.vector
            def _(dve):
                dve.wait_ge(bias_in, 48)
                nc.vector.tensor_reduce(bias_sum[:], bias[:], AX_X, ALU.add).then_inc(step, 1)
                nc.vector.tensor_tensor(y[:], lin_sum[:], dnn_sum[:], ALU.add).then_inc(step, 1)
                dve.wait_ge(step, 2)
                nc.vector.tensor_tensor(y[:], y[:], att_sum[:], ALU.add).then_inc(step, 1)
                dve.wait_ge(step, 3)
                nc.vector.tensor_scalar(y[:], y[:], bias_sum[:, 0:1], None, ALU.add).then_inc(step, 1)

            @block.tensor
            def _(pe):
                pe.wait_ge(step, 4)
                nc.tensor.transpose(ps[:], y[:], ident[:]).then_inc(y_turned, 1)

            @block.scalar
            def _(act):
                act.wait_ge(y_turned, 1)
                nc.scalar.activation(yT[:], ps[:], ACT.Sigmoid).then_inc(y_ready, 1)


def lay_out(inputs):
    g = {k.replace("L0_rec_", ""): np.asarray(v) for k, v in inputs.items()}
    c = np.ascontiguousarray
    NS, ROWS, _ = g["sparse_embed"].shape
    ND = g["dense_embed"].shape[0]
    F = ND + NS
    a = {
        "dense": g["r_dense_input"], "sparse": g["r_sparse_input"],
        "table": g["sparse_embed"].reshape(NS * ROWS, E), "embed": g["dense_embed"].reshape(-1),
        "lin_w": np.pad(g["lin_w"].reshape(-1), (0, -F * E % P)).reshape(-1, P).T, "lin_b": g["lin_b"],
        "table_base": np.arange(NS, dtype=np.float32) * ROWS,
    }
    for pre, mine in (("dnn", "dnn"), ("att_dnn", "att")):
        w0 = g[f"{pre}_w0"]
        if mine == "att":
            w0 = w0.reshape(-1, F, HALVES, QUADS, D).transpose(0, 3, 4, 2, 1).reshape(-1, F * E)
        a[mine + "_w0"], a[mine + "_w1"], a[mine + "_w2"] = w0.T, g[f"{pre}_w1"].T, g[f"{pre}_w2"].T
        a[mine + "_out_w"] = g[f"{pre}_out_w"].reshape(-1, P).T
        a[mine + "_out_b"] = g[f"{pre}_out_b"]
        for n in range(3):
            a[f"{mine}_b{n}"] = g[f"{pre}_b{n}"].reshape(-1, P).T
    for name in ("att_wq", "att_wv", "att_wr"):
        w = g[name]
        t = w.reshape(LAYERS, HALVES, QUADS, D, HALVES, QUADS, D).transpose(5, 6, 0, 4, 1, 2, 3)
        t = np.broadcast_to(t[:, None, :, :, :, :, :, None, :],
                            (QUADS, LANES, D, LAYERS, HALVES, HALVES, QUADS, LANES, D))
        a[name] = t.reshape(P, -1)
    a.update(constants(F))
    return {k: c(v) for k, v in a.items()}


def kernel(**inputs):
    import concourse.bacc as bacc
    from concourse.bass_utils import run_bass_kernel_spmd

    arrays = lay_out(inputs)
    nc = bacc.Bacc("TRN2", target_bir_lowering=False, num_devices=1)
    aps = {k: nc.dram_tensor(f"in_{k}", v.shape, mybir.dt.from_np(v.dtype), kind="ExternalInput").ap()
           for k, v in arrays.items()}
    B = arrays["dense"].shape[0]
    out = nc.dram_tensor("out_y", (B,), F32, kind="ExternalOutput").ap()
    build_kernel(nc, aps, out)
    r = run_bass_kernel_spmd(nc, [{f"in_{k}": v for k, v in arrays.items()}], core_ids=[0])
    return r.results[0]["out_y"]
```

```python
from contextlib import ExitStack

import numpy as np
import concourse.bass as bass
from concourse import mybir

F32 = mybir.dt.float32
F32R = mybir.dt.float32r
I32 = mybir.dt.int32
ALU = mybir.AluOpType
ACT = mybir.ActivationFunctionType
AX_X = mybir.AxisListType.X

P = 128
E = 64
H = 8
D = 8
HALVES = 2
QUADS = 4
LAYERS = 3
PACK = 3
LANES = 4
GROUPS = 8
CHUNK = GROUPS * PACK
STREAMS = 3
STEP = STREAMS * CHUNK
ROUNDS = 4
BEHIND = 2 * CHUNK
BATCH = 256


def constants(F):
    T = PACK * F
    p = np.arange(P)
    lane = (p // D) % LANES
    c = {}
    c["ident"] = np.eye(P)
    c["same_sample"] = (lane[:, None] == lane[None, :]) & (lane[:, None] < PACK)
    c["is_sample"] = lane[:, None] == np.arange(PACK)[None, :]
    c["minus_diag"] = -1.0 * ((p % F)[:, None] == np.arange(F)[None, :])
    ones = (p // F)[:, None] == (p // F)[None, :]
    c["ones_block"] = ones
    sample = p // F
    v = np.zeros((P, D))
    for s in range(PACK):
        v[:, s] = sample == s
    v[:, PACK] = sample == 0
    c["sum_columns"] = v
    return {k: np.ascontiguousarray(a, dtype=np.float32) for k, a in c.items()}


def build_kernel(nc, a, out):
    B = a["dense"].shape[0]
    ND, NS = a["dense"].shape[1], a["sparse"].shape[1]
    F = ND + NS
    K0 = F * E
    TILES = B // P
    STEPS = -(-B // STEP)
    x_dram = nc.dram_tensor("x_rows", ((STEPS + 1) * STEP, K0), F32, kind="Internal").ap()
    att_dram = nc.dram_tensor("att_rows", (STEPS * STEP + BEHIND, K0), F32, kind="Internal").ap()

    with ExitStack() as whole:
        sb = lambda name, shape, dt=F32: whole.enter_context(nc.sbuf_tensor(name, shape, dt))
        sem = lambda name: whole.enter_context(nc.semaphore(name))
        lin_sum = sb("lin_sum", [P, TILES])
        dnn_sum = sb("dnn_sum", [P, TILES])
        att_sum = sb("att_sum", [P, TILES])
        ident = sb("ident", [P, P])

        def clear(sems):
            with nc.Block() as block:
                @block.sync
                def _(sp):
                    for s in sems[0::4]:
                        sp.sem_clear(s)

                @block.scalar
                def _(act):
                    for s in sems[1::4]:
                        act.sem_clear(s)

                @block.vector
                def _(dve):
                    for s in sems[2::4]:
                        dve.sem_clear(s)

                @block.tensor
                def _(pe):
                    for s in sems[3::4]:
                        pe.sem_clear(s)

        dnn_stage(nc, sem, a, "dnn", x_dram, 0, dnn_sum, ident, clear, lin_sum)
        attention_stage(nc, sem, a, x_dram, att_dram, ident, clear, F, K0, STEPS)
        dnn_stage(nc, sem, a, "att", att_dram, BEHIND, att_sum, ident, clear, None)
        finish_stage(nc, a, out, lin_sum, dnn_sum, att_sum, ident, TILES)


def dnn_stage(nc, sem, a, pre, rows_dram, first_row, total, ident, clear, lin_sum):
    gathers = lin_sum is not None
    B, ND = a["dense"].shape
    NS = a["sparse"].shape[1]
    ROWS = a["table"].shape[0] // NS
    K0, H1 = a[pre + "_w0"].shape
    H2, H3 = a[pre + "_w1"].shape[1], a[pre + "_w2"].shape[1]
    TILES = B // P
    KC = -(-K0 // P)
    KL = K0 - (KC - 1) * P
    KH = KC // 2
    HI, LO = 0, 1
    PRODUCTS = ((HI, HI), (LO, HI), (HI, LO))
    Q = BATCH // P
    BATCHES = B // BATCH
    TILES1, TILES2, TILES3 = H1 // P, H2 // P, H3 // P
    with ExitStack() as ctx:
        sb = lambda name, shape, dt=F32: ctx.enter_context(nc.sbuf_tensor(f"{pre}_{name}", shape, dt))
        psum = lambda name, shape: ctx.enter_context(nc.psum_tensor(f"{pre}_{name}", shape, F32))
        w0 = sb("w0_sb", [P, KC, H1])
        w1 = sb("w1_sb", [P, TILES1, H2])
        w2 = sb("w2_sb", [P, TILES2, H3])
        w3 = sb("w3_sb", [P, TILES3])
        biases = [sb(f"b{n}_sb", [P, w // P]) for n, w in enumerate((H1, H2, H3))]
        x = sb("x", [P, Q, K0])
        xT = sb("xT", [P, 2, KC, BATCH], F32R)
        w_part = sb("w_part", [P, 2, 2, KH, P], F32R)
        h0 = sb("h0", [P, TILES1, BATCH])
        h1 = sb("h1", [P, TILES2, BATCH])
        h = [h0, h1, h0]
        psT = psum("psT", [P, 3, 2, BATCH])
        banks = psum("ps", [P, 4, 512])
        ps = banks[:, :, 0:BATCH]
        psY = psum("psY", [P, 2, Q])
        w0_in = [sem(f"{pre}_w0_in{t}") for t in range(TILES1)]
        biases_in = sem(f"{pre}_biases_in")
        rest_in = sem(f"{pre}_rest_in")
        w_hi = sem(f"{pre}_w_hi")
        w_ready = sem(f"{pre}_w_ready")
        half_done = sem(f"{pre}_half_done")
        pad_set = sem(f"{pre}_pad_set")
        turned = sem(f"{pre}_turned")
        x_hi = sem(f"{pre}_x_hi")
        copied = sem(f"{pre}_copied")
        product = sem(f"{pre}_product")
        relued = sem(f"{pre}_relued")
        y_done = sem(f"{pre}_y_done")
        y_out = sem(f"{pre}_y_out")
        sems = [w_hi, w_ready, half_done, turned, x_hi, copied, product, relued, y_done, y_out]
        if gathers:
            rows = sb("rows", [P, TILES, NS], I32)
            rows_now = sb("rows_now", [P, Q, NS], I32)
            base = sb("table_base", [P, NS])
            dense = sb("dense_in", [P, TILES, ND])
            lin_w = sb("lin_w", [P, KC])
            lin_acc = sb("lin_acc", [P, BATCH])
            ones = sb("ones", [P, 1])
            embed = h1[:].rearrange("p c n -> p (c n)")[:, 0:ND * E]
            count = TILES * NS
            idx_in = h1[:].rearrange("p c n -> p (c n)")[:, 0:count].bitcast(I32).rearrange("p (t n) -> p t n", n=NS)
            idx_f, wrap = (h0[:].rearrange("p c n -> p (c n)")[:, k * count:(k + 1) * count].rearrange(
                "p (t n) -> p t n", n=NS) for k in range(2))
            small_in = sem("small_in")
            zeros_ready = sem("zeros_ready")
            zeros_stored = sem("zeros_stored")
            idx_step = sem("idx_step")
            rows_ready = sem("rows_ready")
            gathered = [sem(f"gathered{q}") for q in range(Q)]
            embed_in = sem("embed_in")
            dense_done = sem("dense_done")
            lin_step = sem("lin_step")
            x_stored = sem("x_stored")
            sems += [rows_ready, embed_in, dense_done, lin_step, x_stored]
            GATHER = 16 * NS
        else:
            x_in = [sem(f"{pre}_x_in{q}") for q in range(Q)]
            sems += x_in

        def load_weights(eng):
            full = K0 // P
            for t in range(TILES1):
                cols = slice(t * P, (t + 1) * P)
                eng.dma_start(w0[:, 0:full, cols], a[pre + "_w0"][0:full * P, cols].rearrange("(c p) n -> p c n", p=P)) \
                   .then_inc(w0_in[t], 16)
                eng.dma_start(w0[0:KL, full, cols], a[pre + "_w0"][full * P:K0, cols]).then_inc(w0_in[t], 16)
                if t == 0:
                    for n in range(3):
                        eng.dma_start(biases[n][:], a[f"{pre}_b{n}"]).then_inc(biases_in, 16)
            eng.dma_start(w1[:], a[pre + "_w1"].rearrange("(c p) n -> p c n", p=P)).then_inc(rest_in, 16)
            eng.dma_start(w2[:], a[pre + "_w2"].rearrange("(c p) n -> p c n", p=P)).then_inc(rest_in, 16)
            eng.dma_start(w3[:], a[pre + "_out_w"]).then_inc(rest_in, 16)
        BIASES = REST = 48

        def load_rows(sp, n):
            for q in range(Q):
                sp.dma_start(x[:, q, :], rows_dram[bass.ds(n * BATCH + first_row + q * P, P), :]).then_inc(x_in[q], 16)

        def gather(pool):
            pool.wait_ge(rows_ready, 1)
            for q in range(Q):
                for n in range(NS):
                    nc.gpsimd.indirect_dma_start(
                        out=x[:, q, (ND + n) * E:(ND + n + 1) * E], out_offset=None, in_=a["table"],
                        in_offset=bass.IndirectOffsetOnAxis(ap=rows_now[:, q, n:n + 1], axis=0)) \
                      .then_inc(gathered[q], 16)

        def dense_rows(dve, n):
            nc.vector.tensor_copy(rows_now[:], rows[:, bass.ds(n * Q, Q), :]).then_inc(rows_ready, 1)
            dve.wait_ge(embed_in, 16)
            for q in range(Q):
                dense_q = dense[:, bass.ds(n * Q + q, 1), :].rearrange("p t n -> p (t n)")
                nc.vector.tensor_tensor(x[:, q, 0:ND * E].rearrange("p (f e) -> p f e", e=E),
                                        embed.rearrange("p (f e) -> p f e", e=E),
                                        dense_q.unsqueeze(2).to_broadcast([P, ND, E]), ALU.mult) \
                  .then_inc(dense_done, 1)

        def linear(dve, step):
            c, part = step // 2, step % 2
            k = P if c < KC - 1 else KL
            src = xT[0:k, part, c, :].bitcast(F32)
            if step == 0:
                nc.vector.tensor_scalar(lin_acc[:], src, lin_w[:, 0:1], None, ALU.mult).then_inc(lin_step, 1)
            else:
                dve.wait_ge(lin_step, step)
                nc.vector.scalar_tensor_tensor(out=lin_acc[0:k, :], in0=src, scalar=lin_w[0:k, c:c + 1],
                                               in1=lin_acc[0:k, :], op0=ALU.mult, op1=ALU.add).then_inc(lin_step, 1)
        LIN_STEPS = 2 * KC

        def linear_sum(pe):
            pe.wait_ge(lin_step, LIN_STEPS)
            for q in range(Q):
                nc.tensor.matmul(psY[:, 1, q:q + 1], lin_acc[:, q * P:(q + 1) * P], ones[:], start=True, stop=True)

        def load_embed(sp):
            sp.dma_start(embed, a["embed"].partition_broadcast(P)).then_inc(embed_in, 16)

        def store_rows(sp, n):
            for q in range(Q):
                sp.wait_ge(gathered[q], n * GATHER + GATHER)
                sp.wait_ge(dense_done, q + 1)
                sp.dma_start(rows_dram[bass.ds(n * BATCH + q * P, P), :], x[:, q, :]).then_inc(x_stored, 16)
            sp.wait_ge(x_stored, 16 * Q)

        def turn_rows(pe, n, pair):
            if pair >= 3:
                pe.wait_ge(copied, pair - 2)
            for c in (2 * pair, 2 * pair + 1):
                k = P if c < KC - 1 else KL
                for q in range(Q):
                    if c == 0 and gathers:
                        pe.wait_ge(gathered[q], n * GATHER + GATHER)
                        pe.wait_ge(dense_done, q + 1)
                    elif c == 0:
                        pe.wait_ge(x_in[q], 16)
                    last = nc.tensor.transpose(psT[0:k, pair % 3, c % 2, q * P:(q + 1) * P],
                                               x[:, q, c * P:c * P + k], ident[:])
            last.then_inc(turned, 1)

        def parts_of(pair):
            if pair < KH - 1:
                return ((P, slice(2 * pair, 2 * pair + 2), slice(0, 2)),)
            return tuple((k, slice(2 * pair + c, 2 * pair + c + 1), slice(c, c + 1)) for c, k in enumerate((P, KL)))

        def high_rows(act, pair):
            act.wait_ge(turned, pair + 1)
            for k, to, c in parts_of(pair):
                last = nc.scalar.activation(xT[0:k, HI, to, :], psT[0:k, pair % 3, c, :], ACT.Copy)
            last.then_inc(x_hi, 1)

        def low_rows(dve, pair):
            dve.wait_ge(x_hi, pair + 1)
            for k, to, c in parts_of(pair):
                last = nc.vector.tensor_tensor(xT[0:k, LO, to, :], psT[0:k, pair % 3, c, :],
                                               xT[0:k, HI, to, :].bitcast(F32), ALU.subtract)
            last.then_inc(copied, 1)

        def pad_weights():
            nc.gpsimd.memset(w0[KL:P, KC - 1, :], 0.0).then_inc(pad_set, 1)

        PIECES = 2 * TILES1

        def raw_piece(i):
            t, j = i % PIECES // 2, i % 2
            return w0[:, j * KH:(j + 1) * KH, t * P:(t + 1) * P]

        def high_piece(act, i):
            act.wait_ge(w0_in[i % PIECES // 2], 32)
            nc.scalar.activation(w_part[:, i % 2, HI], raw_piece(i), ACT.Copy).then_inc(w_hi, 1)

        def low_piece(i):
            nc.vector.tensor_tensor(w_part[:, i % 2, LO], raw_piece(i), w_part[:, i % 2, HI].bitcast(F32),
                                    ALU.subtract).then_inc(w_ready, 1)

        def body(n, last_turn):
            ahead = 0 if last_turn else 2
            turns = [[] for _ in range(TILES2 + TILES3)]
            if not last_turn:
                for pair in range(KH):
                    turns[max(0, (pair - 1) // 2)].append(pair)
            with nc.Block() as block:
                @block.sync
                def _(sp):
                    if not last_turn and gathers:
                        load_embed(sp)
                        store_rows(sp, n + 1)
                    elif not last_turn:
                        load_rows(sp, n + 1)

                if gathers and not last_turn:
                    @block.gpsimd
                    def _(pool):
                        gather(pool)

                @block.tensor
                def _(pe):
                    for i in range(PIECES):
                        t, j = i // 2, i % 2
                        if i >= 2:
                            pe.wait_ge(w_ready, i - 1)
                        if t >= 4 and j == 0:
                            pe.wait_ge(relued, t - 3)
                        for c in range(j * KH, (j + 1) * KH):
                            k = KL if c == KC - 1 else P
                            for m, (wp, xp) in enumerate(PRODUCTS):
                                last = nc.tensor.matmul(ps[:, t % 4, :], w_part[0:k, i % 2, wp, c - j * KH, :],
                                                        xT[0:k, xp, c, :], start=(c == 0 and m == 0),
                                                        stop=(c == KC - 1 and m == 2))
                        last.then_inc(product if j else half_done, 1)
                    tile = TILES1
                    for layer, w, kc, tiles in ((1, w1, TILES1, TILES2), (2, w2, TILES2, TILES3)):
                        src = h[layer - 1]
                        for t in range(tiles):
                            for pair in turns[tile - TILES1]:
                                turn_rows(pe, n + 1, pair)
                            if tile == TILES1:
                                pe.wait_ge(rest_in, REST)
                            if t == 0:
                                pe.wait_ge(relued, tile)
                            else:
                                pe.wait_ge(relued, tile - 3)
                            for c in range(kc):
                                last = nc.tensor.matmul(ps[:, tile % 4, :], w[:, c, t * P:(t + 1) * P],
                                                        src[:, c, :], start=(c == 0), stop=(c == kc - 1))
                            last.then_inc(product, 1)
                            tile += 1
                    if gathers:
                        linear_sum(pe)
                    pe.wait_ge(relued, tile)
                    for q in range(Q):
                        for c in range(TILES3):
                            last = nc.tensor.matmul(psY[:, 0, q:q + 1], h[2][:, c, q * P:(q + 1) * P], w3[:, c:c + 1],
                                                    start=(c == 0), stop=(c == TILES3 - 1))
                    last.then_inc(y_done, 1)

                @block.scalar
                def _(act):
                    def relu(layer, tile, t):
                        act.wait_ge(product, tile + 1)
                        nc.scalar.activation(h[layer][:, t, :], ps[:, tile % 4, :], ACT.Relu,
                                             bias=biases[layer][:, t:t + 1]).then_inc(relued, 1)

                    act.wait_ge(biases_in, BIASES)
                    for i in range(2, PIECES + ahead):
                        if i % 2:
                            act.wait_ge(product, i // 2)
                        else:
                            act.wait_ge(half_done, i // 2)
                        high_piece(act, i)
                        if i % 2:
                            relu(0, i // 2 - 1, i // 2 - 1)
                    if last_turn:
                        relu(0, TILES1 - 1, TILES1 - 1)
                    tile = TILES1
                    for layer, tiles in ((1, TILES2), (2, TILES3)):
                        for t in range(tiles):
                            for pair in turns[tile - TILES1]:
                                high_rows(act, pair)
                            if tile == TILES1 and gathers and not last_turn:
                                act.wait_ge(dense_done, Q)
                            if layer == 2 and t == 0:
                                act.wait_ge(product, TILES1 + TILES2)
                            relu(layer, tile, t)
                            tile += 1

                @block.vector
                def _(dve):
                    if not last_turn and gathers:
                        dense_rows(dve, n + 1)
                    steps = list(range(LIN_STEPS)) if gathers else []
                    for i in range(2, PIECES + ahead):
                        dve.wait_ge(w_hi, i - 1)
                        low_piece(i)
                        for step in steps[3 * (i - 2):3 * (i - 1)]:
                            linear(dve, step)
                    if not last_turn:
                        for pair in range(KH):
                            low_rows(dve, pair)
                    dve.wait_ge(y_done, 1)
                    nc.vector.tensor_copy(total[:, bass.ds(n * Q, Q)], psY[:, 0, :]).then_inc(y_out, 1)
                    if gathers:
                        nc.vector.tensor_copy(lin_sum[:, bass.ds(n * Q, Q)], psY[:, 1, :]).then_inc(y_out, 1)
            clear(sems)

        if gathers:
            with nc.Block() as block:
                @block.sync
                def _(sp):
                    sp.dma_start(idx_in, a["sparse"].rearrange("(t p) n -> p t n", p=P)).then_inc(small_in, 16)
                    sp.dma_start(dense[:], a["dense"].rearrange("(t p) n -> p t n", p=P)).then_inc(small_in, 16)
                    sp.dma_start(base[:], a["table_base"].partition_broadcast(P)).then_inc(small_in, 16)
                    sp.dma_start(lin_w[:], a["lin_w"]).then_inc(small_in, 16)
                    sp.dma_start(ident[:], a["ident"]).then_inc(small_in, 16)
                    sp.wait_ge(zeros_ready, 1)
                    pieces = range(B, rows_dram.shape[0], P)
                    for row in pieces:
                        count = min(P, rows_dram.shape[0] - row)
                        sp.dma_start(rows_dram[row:row + count, :], x[0:count, 0, :]).then_inc(zeros_stored, 16)
                    sp.wait_ge(zeros_stored, 16 * len(pieces))

                @block.scalar
                def _(act):
                    load_weights(act)

                @block.gpsimd
                def _(pool):
                    pad_weights()

                @block.vector
                def _(dve):
                    nc.vector.memset(x[:, 0, :], 0.0).then_inc(zeros_ready, 1)
                    nc.vector.memset(ones[:], 1.0).then_inc(idx_step, 1)
                    dve.wait_ge(small_in, 80)
                    nc.vector.tensor_copy(idx_f, idx_in).then_inc(idx_step, 1)
                    dve.wait_ge(idx_step, 2)
                    nc.vector.tensor_scalar(wrap, idx_f, 0.0, float(ROWS), ALU.is_lt, ALU.mult).then_inc(idx_step, 1)
                    dve.wait_ge(idx_step, 3)
                    nc.vector.tensor_tensor(idx_f, idx_f, wrap, ALU.add).then_inc(idx_step, 1)
                    dve.wait_ge(idx_step, 4)
                    nc.vector.tensor_scalar(wrap, idx_f, 0.0, float(ROWS - 1), ALU.max, ALU.min) \
                      .then_inc(idx_step, 1)
                    dve.wait_ge(idx_step, 5)
                    nc.vector.tensor_tensor(rows[:], wrap, base[:].unsqueeze(1).to_broadcast([P, TILES, NS]),
                                            ALU.add).then_inc(idx_step, 1)
                    dve.wait_ge(idx_step, 6)
            with nc.Block() as block:
                @block.gpsimd
                def _(pool):
                    gather(pool)

                @block.sync
                def _(sp):
                    load_embed(sp)
                    store_rows(sp, 0)

                @block.tensor
                def _(pe):
                    for pair in range(KH):
                        turn_rows(pe, 0, pair)

                @block.scalar
                def _(act):
                    for i in range(2):
                        high_piece(act, i)
                    for pair in range(KH):
                        high_rows(act, pair)

                @block.vector
                def _(dve):
                    dense_rows(dve, 0)
                    for i in range(2):
                        dve.wait_ge(w_hi, i + 1)
                        low_piece(i)
                    for pair in range(KH):
                        low_rows(dve, pair)
        else:
            with nc.Block() as block:
                @block.sync
                def _(sp):
                    load_rows(sp, 0)

                @block.scalar
                def _(act):
                    load_weights(act)
                    act.wait_ge(pad_set, 1)
                    for i in range(2):
                        high_piece(act, i)
                    for pair in range(KH):
                        high_rows(act, pair)

                @block.tensor
                def _(pe):
                    for pair in range(KH):
                        turn_rows(pe, 0, pair)

                @block.gpsimd
                def _(pool):
                    pad_weights()

                @block.vector
                def _(dve):
                    for i in range(2):
                        dve.wait_ge(w_hi, i + 1)
                        low_piece(i)
                    for pair in range(KH):
                        low_rows(dve, pair)
        clear(sems)
        if BATCHES > 1:
            with nc.Fori(0, BATCHES - 1) as n:
                body(n, False)
        body(BATCHES - 1, True)


def attention_stage(nc, sem, a, x_dram, att_dram, ident, clear, F, K0, STEPS):
    T = PACK * F
    HF = GROUPS * F
    HC = QUADS * F
    SCALE = float(D) ** -0.5
    PAIR = 2
    PT = PAIR * F
    TT = GROUPS // PAIR
    SPLIT = 3
    HS = HF // SPLIT
    PIECES = HALVES * SPLIT
    UNITS = LAYERS * STREAMS
    WT = LAYERS * HALVES * HALVES
    HI, LO = 0, 1
    PRODUCTS = ((HI, HI), (HI, LO), (LO, HI))
    with ExitStack() as ctx:
        sb = lambda name, shape, dt=F32: ctx.enter_context(nc.sbuf_tensor(name, shape, dt))
        psum = lambda name, shape: ctx.enter_context(nc.psum_tensor(name, shape, F32))
        wq, wv, wr = (sb(n, [P, 2, LAYERS, HALVES, HALVES, P], F32R) for n in ("wq", "wv", "wr"))
        is_sample = sb("is_sample", [P, PACK])
        minus_diag = sb("minus_diag", [P, F])
        ones_block = sb("ones_block", [P, P], F32R)
        v_sb = sb("v_sb", [T, GROUPS, H, 32])
        o_sb = sb("o_sb", [P, HALVES, HF])
        xt = [sb(f"xt{s}", [PT, TT, PACK, E]) for s in range(STREAMS)]
        xL = [sb(f"xL{s}", [P, 2, HALVES, HF], F32R) for s in range(STREAMS)]
        q_bd = [sb(f"q_bd{s}", [P, HALVES, GROUPS, T]) for s in range(STREAMS)]
        q_heads = [sb(f"q_heads{s}", [P, HALVES, GROUPS, QUADS, F]) for s in range(STREAMS)]
        x_perm = sb("x_perm", [PT, TT, HALVES, P])
        recips_wide = sb("recips_wide", [HS, PIECES, P])
        psP = psum("psP", [P, HALVES, 512])
        psO = psum("psO", [P, HALVES, 512])
        psS = psum("psS", [P, 3, 512])
        psV = psum("psV", [P, 512])

        consts_in = sem("consts_in")
        consts_step = sem("consts_step")
        consts_ready = sem("consts_ready")

        with ExitStack() as early:
            raw = {n: early.enter_context(nc.sbuf_tensor(n + "_raw", [P, WT, P], F32)) for n in ("wq", "wv", "wr")}
            ones_raw = early.enter_context(nc.sbuf_tensor("ones_raw", [P, P], F32))
            same_sample = early.enter_context(nc.sbuf_tensor("same_sample", [P, P], F32))
            sum_columns = early.enter_context(nc.sbuf_tensor("sum_columns", [P, D], F32))
            with nc.Block() as block:
                @block.sync
                def _(sp):
                    for dst, name in ((same_sample, "same_sample"), (ones_raw, "ones_block"),
                                      (sum_columns, "sum_columns"), (is_sample, "is_sample"),
                                      (minus_diag, "minus_diag")):
                        sp.dma_start(dst[:], a[name]).then_inc(consts_in, 16)
                    for n in ("wq", "wv", "wr"):
                        sp.dma_start(raw[n][:].rearrange("p t n -> p (t n)"), a["att_" + n]).then_inc(consts_in, 16)

                @block.gpsimd
                def _(pool):
                    nc.gpsimd.memset(x_perm[:], 0.0).then_inc(consts_ready, 1)
                    nc.gpsimd.memset(xL[STREAMS - 1][:].bitcast(F32), 0.0).then_inc(consts_ready, 1)
                    for s in range(STREAMS):
                        nc.gpsimd.memset(q_heads[s][:], 0.0).then_inc(consts_ready, 1)

                @block.vector
                def _(dve):
                    nc.vector.memset(o_sb[:], 1.0).then_inc(consts_ready, 1)
                    nc.vector.memset(psO[:], 1.0).then_inc(consts_ready, 1)
                    dve.wait_ge(consts_in, 128)
                    for k, (n, w) in enumerate((("wq", wq), ("wv", wv), ("wr", wr))):
                        w_hi, w_lo = (w[:, part].rearrange("p l i o n -> p (l i o) n") for part in (HI, LO))
                        nc.vector.tensor_tensor(raw[n][:], raw[n][:], same_sample[:].unsqueeze(1).to_broadcast(
                            [P, WT, P]), ALU.mult).then_inc(consts_step, 1)
                        dve.wait_ge(consts_step, 2 * k + 1)
                        nc.vector.tensor_copy(w_hi, raw[n][:]).then_inc(consts_step, 1)
                        dve.wait_ge(consts_step, 2 * k + 2)
                        nc.vector.tensor_tensor(w_lo, raw[n][:], w_hi.bitcast(F32), ALU.subtract) \
                          .then_inc(consts_ready, 1)
                    nc.vector.tensor_copy(ones_block[:], ones_raw[:]).then_inc(consts_ready, 1)
                    nc.vector.tensor_copy(
                        v_sb[:, :, :, PACK * D:32].rearrange("p g h c -> p (g h) c"),
                        sum_columns[0:T, :].unsqueeze(1).to_broadcast([T, GROUPS * H, D])).then_inc(consts_ready, 1)
        m = sb("m", [T, 4, H])
        m_hi = sb("m_hi", [T, 4, H], F32R)
        m_lo = sb("m_lo", [T, 4, H])
        m_diag = sb("m_diag", [T, 3, 2, H, F], F32R)
        e_sb = sb("e_sb", [T, 3, H, F])
        recips = sb("recips", [HS, PIECES, QUADS * LANES])
        mixed = sb("mixed", [P, HALVES, HF])
        q_sb = sb("q_sb", [P, HALVES, HF])
        v_lanes = sb("v_lanes", [P, HALVES, HF])
        v_bd = [sb(f"v_bd{s}", [P, HALVES, GROUPS, T]) for s in range(STREAMS)]
        x_out = sb("x_out", [P, GROUPS, HALVES, F])

        xt_in = [sem(f"xt_in{s}") for s in range(STREAMS)]
        permuted = sem("permuted")
        widened = sem("widened")
        turned = sem("rows_turned")
        taken_hi = sem("taken_hi")
        taken_lo = sem("taken_lo")
        hi_ready = sem("hi_ready")
        lo_ready = sem("lo_ready")
        q_done = sem("q_done")
        q_copied = sem("q_copied")
        q_spread = sem("q_spread")
        vals_done = sem("vals_done")
        vals_copied = sem("vals_copied")
        vals_spread = sem("vals_spread")
        v_done = sem("v_done")
        v_copied = sem("v_copied")
        s_done = sem("s_done")
        max_done = sem("max_done")
        hi_done = sem("max_hi_done")
        rest_done = sem("max_rest_done")
        diag_ready = sem("diag_ready")
        shifted = sem("shifted")
        exp_done = sem("exp_done")
        mix_done = sem("mix_done")
        o_copied = sem("o_copied")
        sums_turned = sem("sums_turned")
        recip_done = sem("recip_done")
        recip_back = sem("recip_back")
        normed = sem("normed")
        res_done = sem("res_done")
        res_added = sem("res_added")
        stored = sem("stored")
        x_out_set = sem("x_out_set")
        sems = xt_in + [taken_hi, taken_lo, permuted, widened, turned, hi_ready, lo_ready,
                        q_done, q_copied, q_spread, vals_done, vals_copied, vals_spread, v_done,
                        v_copied, s_done, max_done, hi_done, rest_done, diag_ready, shifted,
                        exp_done, mix_done, o_copied, sums_turned, recip_done, recip_back,
                        normed, res_done, res_added]

        def load_xt(eng, s, row):
            for t in range(TT):
                for g in range(PAIR):
                    src = x_dram[bass.ds(row + PACK * (t * PAIR + g), PACK), :].rearrange("s (f e) -> f s e", e=E)
                    eng.dma_start(xt[s][g * F:(g + 1) * F, t, :, :], src).then_inc(xt_in[s], 16)
        XT = 16 * TT * PAIR

        def store_out(sp, row):
            for q in range(QUADS):
                for k in range(PACK):
                    dst = att_dram[bass.ds(row, CHUNK), :].rearrange("(g s) n -> s g n", s=PACK)[k].rearrange(
                        "g (q d c) -> q d g c", q=QUADS, d=D)[q]
                    sp.dma_start(dst, x_out[32 * q + D * k:32 * q + D * (k + 1), :, :, :].rearrange(
                        "p g h f -> p g (h f)")).then_inc(stored, 16)
        STORE = 16 * QUADS * PACK

        def pe_turn(pe):
            for hf in range(HALVES):
                for t in range(TT):
                    last = nc.tensor.transpose(psP[:, hf, t * PT:(t + 1) * PT], x_perm[:, t, hf, :],
                                               ident[0:PT, 0:PT])
            last.then_inc(turned, 1)

        def pe_project(pe, s, w, layer, done, halves=range(HALVES)):
            for ho in halves:
                steps = [(hi, wp, xp) for wp, xp in PRODUCTS for hi in range(HALVES)]
                for n, (hi, wp, xp) in enumerate(steps):
                    last = nc.tensor.matmul(psP[:, ho, 0:HF], w[:, wp, layer, hi, ho, :], xL[s][:, xp, hi, :],
                                            start=(n == 0), stop=(n == len(steps) - 1))
            if ho == HALVES - 1:
                last.then_inc(done, 1)

        def pe_values(pe, s, pair):
            for j in range(PAIR):
                for hf in range(HALVES):
                    last = nc.tensor.transpose(psV[0:T, (j * HALVES + hf) * P:(j * HALVES + hf + 1) * P],
                                               v_bd[s][:, hf, pair * PAIR + j, :], ident[:])
            last.then_inc(v_done, 1)

        def pe_turn_sums(pe):
            for hf in range(HALVES):
                for c in range(SPLIT):
                    last = nc.tensor.transpose(psP[0:HS, hf, c * P:(c + 1) * P],
                                               o_sb[:, hf, c * HS:(c + 1) * HS], ident[:])
            last.then_inc(sums_turned, 1)

        def pe_turn_back(pe):
            for hf in range(HALVES):
                for c in range(SPLIT):
                    last = nc.tensor.transpose(psP[:, hf, c * HS:(c + 1) * HS], recips_wide[:, hf * SPLIT + c, :],
                                               ident[0:HS, 0:HS])
            last.then_inc(recip_back, 1)

        def dve_recip(dve):
            for hf in range(HALVES):
                src = psP[0:HS, hf, 0:SPLIT * P].rearrange("p (c r) -> p c r", r=32)[:, :, PACK * D:PACK * D + LANES]
                last = nc.vector.reciprocal(recips[:, hf * SPLIT:(hf + 1) * SPLIT, :].rearrange(
                    "p c (q r) -> p (c q) r", q=QUADS), src)
            last.then_inc(recip_done, 1)

        def act_widen(act):
            nc.scalar.activation(recips_wide.rearrange("p c (r d) -> p c r d", d=D),
                                 recips[:].unsqueeze(3).to_broadcast([HS, PIECES, QUADS * LANES, D]), ACT.Copy) \
              .then_inc(widened, 1)

        def dve_norm(dve):
            nc.vector.tensor_tensor(mixed[:], o_sb[:], psP[:, :, 0:HF], ALU.mult).then_inc(normed, 1)

        def dve_add(dve):
            nc.vector.tensor_tensor(mixed[:], mixed[:], psP[:, :, 0:HF], ALU.add).then_inc(res_added, 1)

        def dve_copy_mixed(dve):
            nc.vector.tensor_copy(o_sb[:], psO[:, :, 0:HF]).then_inc(o_copied, 1)

        def act_relu(act, s, is_out):
            if is_out:
                nc.scalar.activation(x_out[:].rearrange("p g h f -> p h g f"),
                                     mixed[:].rearrange("p h (g f) -> p h g f", f=F), ACT.Relu) \
                  .then_inc(hi_ready, 1)
            else:
                nc.scalar.activation(xL[s][:, HI], mixed[:], ACT.Relu).then_inc(hi_ready, 1)

        def dve_low(dve, s):
            nc.vector.scalar_tensor_tensor(out=xL[s][:, LO], in0=mixed[:], scalar=0.0,
                                           in1=xL[s][:, HI].bitcast(F32), op0=ALU.max, op1=ALU.subtract) \
              .then_inc(lo_ready, 1)

        def act_take(act, s):
            nc.scalar.activation(xL[s][:, HI], psP[:, :, 0:HF], ACT.Copy).then_inc(taken_hi, 1)

        def dve_take_low(dve, s):
            nc.vector.tensor_tensor(xL[s][:, LO], psP[:, :, 0:HF], xL[s][:, HI].bitcast(F32), ALU.subtract) \
              .then_inc(taken_lo, 1)

        def permute(pool, s, t):
            nc.gpsimd.tensor_copy(
                x_perm[:, t, :, :].rearrange("p h (q s d) -> p (h q) s d", s=LANES, d=D)[:, :, 0:PACK, :],
                xt[s][:, t, :, :].rearrange("p s (h d) -> p h s d", d=D)).then_inc(permuted, 1)

        def act_copy_q(act):
            nc.scalar.activation(q_sb[:], psP[:, :, 0:HF], ACT.Copy).then_inc(q_copied, 1)

        def by_group(t):
            return t[:].rearrange("p h (g f) -> p (h g) f", f=F)

        def q_block(eng, s, k):
            return nc.vector.tensor_scalar(q_bd[s][:].rearrange("p h g t -> p (h g) t")[:, :, k * F:(k + 1) * F],
                                           by_group(q_sb), is_sample[:, k:k + 1], None, ALU.mult)

        def q_head(engine, s, k):
            rows = slice(32 * k, 32 * k + 32)
            dst = q_heads[s][rows, :, :, k, :].rearrange("p h g f -> p (h g) f")
            src = q_sb[rows].rearrange("p h (g f) -> p (h g) f", f=F)
            if engine is nc.scalar:
                return nc.scalar.activation(dst, src, ACT.Copy)
            return engine.tensor_copy(dst, src)

        def act_copy_v(act):
            nc.scalar.activation(v_lanes[:], psP[:, :, 0:HF], ACT.Copy).then_inc(vals_copied, 1)

        def value_block(engine, s, k):
            dst = v_bd[s][:].rearrange("p h g t -> p (h g) t")[:, :, k * F:(k + 1) * F]
            if engine is nc.scalar:
                return nc.scalar.activation(dst, by_group(v_lanes), ACT.Copy, scale=is_sample[:, k:k + 1])
            return engine.tensor_scalar(dst, by_group(v_lanes), is_sample[:, k:k + 1], None, ALU.mult)

        def act_copy_values(act, pair):
            nc.scalar.activation(
                v_sb[:, pair * PAIR:(pair + 1) * PAIR, :, 0:PACK * D].rearrange("p g h c -> p (g h) c"),
                psV[0:T, :].rearrange("p (j c) -> p j c", c=32)[:, :, 0:PACK * D],
                ACT.Copy).then_inc(v_copied, 1)

        clear([consts_in])
        with nc.Block() as block:
            @block.sync
            def _(sp):
                for s in range(STREAMS):
                    load_xt(sp, s, s * CHUNK)
                sp.wait_ge(xt_in[STREAMS - 1], XT)

            @block.gpsimd
            def _(pool):
                pool.wait_ge(xt_in[0], XT)
                for t in range(TT):
                    permute(pool, 0, t)
                pool.wait_ge(xt_in[1], XT)
                pool.wait_ge(turned, 1)
                for t in range(TT):
                    permute(pool, 1, t)

            @block.tensor
            def _(pe):
                pe.wait_ge(permuted, TT)
                pe_turn(pe)
                pe.wait_ge(taken_lo, 1)
                pe_project(pe, 0, wq, 0, q_done)
                pe.wait_ge(q_copied, 1)
                pe_project(pe, 0, wv, 0, vals_done)

            @block.scalar
            def _(act):
                act.wait_ge(turned, 1)
                act_take(act, 0)
                act.wait_ge(q_done, 1)
                act_copy_q(act)
                act.wait_ge(q_copied, 1)
                q_head(nc.scalar, 0, 0)
                q_head(nc.scalar, 0, 1).then_inc(q_spread, 1)
                act.wait_ge(vals_done, 1)
                act_copy_v(act)
                act.wait_ge(vals_copied, 1)
                for k in range(PACK):
                    value_block(nc.scalar, 0, k).then_inc(vals_spread, 1)

            @block.vector
            def _(dve):
                nc.vector.memset(x_out[:], 0.0).then_inc(x_out_set, 1)
                dve.wait_ge(taken_hi, 1)
                dve_take_low(dve, 0)
                dve.wait_ge(q_copied, 1)
                for k in range(PACK):
                    q_block(dve, 0, k)
                q_head(nc.vector, 0, 2)
                q_head(nc.vector, 0, 3).then_inc(q_spread, 1)
        clear(sems)

        TURN_X, VALUES, TURN_SUMS, QUERY, TURN_BACK, RESIDUAL = 0, 2, 3, 4, 5, 6
        PAIR_AT = (0, 1, 3, 5)
        PERMUTE = 3
        SHIFT, MIX = 2, 3
        stream = lambda u: u % STREAMS
        layer = lambda u: u // STREAMS % LAYERS
        def pass_chunks(row, stored_before, rounds):
            units = rounds * UNITS
            slots = GROUPS * units
            is_out = [layer(u - 1) == LAYERS - 1 for u in range(units)]
            turns_x = [layer(u + 1) == 0 for u in range(units)]
            assert all(is_out[u - 1] == turns_x[u] for u in range(units))
            outs = lambda u: sum(is_out[:u + 1])
            turned_at = lambda u: sum(turns_x[:u + 1])

            with nc.Block() as block:
                @block.sync
                def _(sp):
                    store_out(sp, row)
                    for s in range(STREAMS - 1):
                        load_xt(sp, s, row + STEP + s * CHUNK)
                    store = 1
                    for u in range(units):
                        if not is_out[u]:
                            continue
                        s, rnd = stream(u + 2), (u + 2) // UNITS
                        if u + UNITS < units or s == STREAMS - 1:
                            sp.wait_ge(permuted, TT * outs(u))
                            load_xt(sp, s, row + (rnd + 1) * STEP + s * CHUNK)
                        if u < units - 1:
                            sp.wait_ge(hi_ready, u + 1)
                            store_out(sp, row + store * CHUNK)
                            store += 1
                    sp.wait_ge(xt_in[STREAMS - 1], XT * rounds)

                @block.tensor
                def _(pe):
                    for n in range(slots + MIX):
                        u, g = n // GROUPS, n % GROUPS
                        s = stream(u)
                        if n < slots:
                            if g == 0 and u:
                                pe.wait_ge(q_spread, 2 * u)
                            if n >= 3:
                                pe.wait_ge(exp_done, n - 2)
                            for hf in range(HALVES):
                                last = nc.tensor.matmul(psS[0:T, n % 3, hf * HC:(hf + 1) * HC],
                                                        q_bd[s][:, hf, g, :], q_heads[s][:, hf, g, :, :],
                                                        start=(hf == 0), stop=False, skip_group_check=True)
                            last.then_inc(s_done, 1)
                        if SHIFT <= n < slots + SHIFT:
                            k = n - SHIFT
                            pe.wait_ge(diag_ready, 2 * (k + 1))
                            for part in (HI, LO):
                                last = nc.tensor.matmul(psS[0:T, k % 3, 0:H * F], ones_block[0:T, 0:T],
                                                        m_diag[:, k % 3, part].rearrange("p h f -> p (h f)"),
                                                        start=False, stop=(part == LO), skip_group_check=True)
                            last.then_inc(shifted, 1)
                        if n >= MIX:
                            mu, mg = (n - MIX) // GROUPS, (n - MIX) % GROUPS
                            if mg == 0 and mu:
                                pe.wait_ge(o_copied, mu)
                            if mg % PAIR == 0:
                                pe.wait_ge(v_copied, TT * mu + mg // PAIR + 1)
                            pe.wait_ge(exp_done, n - MIX + 1)
                            for h in range(H):
                                hf, q = h // QUADS, h % QUADS
                                last = nc.tensor.matmul(
                                    psO[32 * q:32 * q + PACK * (D + 1), hf, mg * F:(mg + 1) * F],
                                    v_sb[:, mg, h, 0:PACK * (D + 1)], e_sb[:, (n - MIX) % 3, h, :],
                                    start=True, stop=True)
                            last.then_inc(mix_done, 1)
                        if n < slots:
                            if g == TURN_X and turns_x[u]:
                                if u:
                                    pe.wait_ge(permuted, TT * turned_at(u - 1))
                                    pe.wait_ge(res_added, u)
                                pe_turn(pe)
                            if g == VALUES:
                                if turns_x[u]:
                                    pe.wait_ge(taken_lo, turned_at(u))
                                else:
                                    pe.wait_ge(lo_ready, u + 1 - turned_at(u))
                                pe_project(pe, stream(u + 1), wv, layer(u + 1), vals_done)
                            if g == TURN_SUMS:
                                if u:
                                    pe.wait_ge(o_copied, u)
                                pe.wait_ge(vals_copied, u + 1)
                                pe_turn_sums(pe)
                            if g == QUERY:
                                pe.wait_ge(recip_done, u + 1)
                                pe_project(pe, stream(u + 1), wq, layer(u + 1), q_done)
                            if g == TURN_BACK:
                                pe.wait_ge(q_copied, u + 1)
                                pe.wait_ge(widened, u + 1)
                                pe_turn_back(pe)
                            if g == RESIDUAL:
                                pe.wait_ge(normed, u + 1)
                            if g >= RESIDUAL:
                                pe_project(pe, stream(u - 1), wr, layer(u - 1), res_done, (g - RESIDUAL,))
                            if g in PAIR_AT:
                                pair = PAIR_AT.index(g)
                                if pair == 0 and u:
                                    pe.wait_ge(vals_spread, PACK * u)
                                if TT * u + pair:
                                    pe.wait_ge(v_copied, TT * u + pair)
                                pe_values(pe, s, pair)

                @block.vector
                def _(dve):
                    for n in range(slots):
                        u, g = n // GROUPS, n % GROUPS
                        dve.wait_ge(s_done, n + 1)
                        if n >= 4:
                            dve.wait_ge(diag_ready, 2 * (n - 3))
                        nc.vector.tensor_reduce(
                            m[:, n % 4, :], psS[0:T, n % 3, 0:H * F].rearrange("p (h f) -> p h f", h=H),
                            AX_X, ALU.max).then_inc(max_done, 1)
                        if g == VALUES + 2:
                            dve.wait_ge(vals_copied, u + 1)
                            value_block(nc.vector, stream(u + 1), 2).then_inc(vals_spread, 1)
                        if g == QUERY + 1:
                            dve.wait_ge(q_copied, u + 1)
                            q_block(dve, stream(u + 1), 0)
                        if g == QUERY + 2:
                            q_block(dve, stream(u + 1), 1)
                            q_block(dve, stream(u + 1), 2)
                        if g == QUERY + 3:
                            q_head(nc.vector, stream(u + 1), 2).then_inc(q_spread, 1)
                        if g == MIX - 1 and u:
                            dve.wait_ge(mix_done, GROUPS * u)
                            dve.wait_ge(normed, u)
                            dve_copy_mixed(dve)
                        dve.wait_ge(max_done, n + 1)
                        nc.vector.tensor_copy(m_hi[:, n % 4, :], m[:, n % 4, :]).then_inc(hi_done, 1)
                        dve.wait_ge(hi_done, n + 1)
                        nc.vector.tensor_tensor(m_lo[:, n % 4, :], m[:, n % 4, :], m_hi[:, n % 4, :].bitcast(F32),
                                                ALU.subtract).then_inc(rest_done, 1)
                        if g == TURN_X and turns_x[u]:
                            dve.wait_ge(taken_hi, turned_at(u))
                            dve_take_low(dve, stream(u + 1))
                        if g == 0 and u and not is_out[u - 1]:
                            dve.wait_ge(hi_ready, u)
                            dve_low(dve, stream(u - 2))
                        if g == TURN_SUMS:
                            dve.wait_ge(sums_turned, u + 1)
                            if u:
                                dve.wait_ge(widened, u)
                            dve_recip(dve)
                        if g == TURN_BACK:
                            dve.wait_ge(recip_back, u + 1)
                            if u:
                                dve.wait_ge(hi_ready, u)
                            dve_norm(dve)
                        if g == RESIDUAL + 1:
                            dve.wait_ge(normed, u + 1)
                            dve.wait_ge(res_done, u + 1)
                            dve_add(dve)
                    dve.wait_ge(mix_done, slots)
                    dve.wait_ge(normed, units)
                    dve_copy_mixed(dve)

                @block.gpsimd
                def _(pool):
                    for n in range(slots):
                        u, g = n // GROUPS, n % GROUPS
                        pool.wait_ge(max_done, n + 1)
                        if n >= 3:
                            pool.wait_ge(shifted, n - 2)
                        for part, src in ((HI, m), (LO, m_lo)):
                            if part == LO:
                                pool.wait_ge(rest_done, n + 1)
                            nc.gpsimd.tensor_tensor(m_diag[:, n % 3, part],
                                                    src[:, n % 4, :].unsqueeze(2).to_broadcast([T, H, F]),
                                                    minus_diag[0:T, :].unsqueeze(1).to_broadcast([T, H, F]),
                                                    ALU.mult).then_inc(diag_ready, 1)
                        if is_out[u] and PERMUTE <= g < PERMUTE + TT:
                            if g == PERMUTE:
                                if u + 2 >= UNITS:
                                    pool.wait_ge(xt_in[stream(u + 2)], XT * ((u + 2) // UNITS))
                                pool.wait_ge(turned, turned_at(u))
                            permute(pool, stream(u + 2), g - PERMUTE)

                @block.scalar
                def _(act):
                    for n in range(slots + SHIFT):
                        u, g = n // GROUPS, n % GROUPS
                        if n >= SHIFT:
                            k = n - SHIFT
                            act.wait_ge(shifted, k + 1)
                            if k >= 3:
                                act.wait_ge(mix_done, k - 2)
                            nc.scalar.activation(e_sb[:, k % 3].rearrange("p h f -> p (h f)"),
                                                 psS[0:T, k % 3, 0:H * F], ACT.Exp, scale=SCALE) \
                              .then_inc(exp_done, 1)
                        if g == 0 and u:
                            act.wait_ge(res_added, u)
                            if is_out[u - 1]:
                                act.wait_ge(stored, stored_before + outs(u - 1) * STORE)
                            act_relu(act, stream(u - 2), is_out[u - 1])
                        if n >= slots:
                            continue
                        ns = stream(u + 1)
                        if g in PAIR_AT:
                            pair = PAIR_AT.index(g)
                            act.wait_ge(v_done, TT * u + pair + 1)
                            if u:
                                act.wait_ge(mix_done, GROUPS * (u - 1) + PAIR * (pair + 1))
                            act_copy_values(act, pair)
                        if g == TURN_X and turns_x[u]:
                            act.wait_ge(turned, turned_at(u))
                            act_take(act, ns)
                        if g == VALUES:
                            act.wait_ge(vals_done, u + 1)
                            if u:
                                act.wait_ge(vals_spread, PACK * u)
                            act_copy_v(act)
                        if g == VALUES + 1:
                            act.wait_ge(vals_copied, u + 1)
                            value_block(nc.scalar, ns, 0).then_inc(vals_spread, 1)
                        if g == TURN_SUMS:
                            act.wait_ge(recip_done, u + 1)
                            if u:
                                act.wait_ge(recip_back, u)
                            act_widen(act)
                        if g == QUERY:
                            act.wait_ge(q_done, u + 1)
                            if u:
                                act.wait_ge(q_spread, 2 * u)
                            act_copy_q(act)
                            value_block(nc.scalar, ns, 1).then_inc(vals_spread, 1)
                        if g == QUERY + 1:
                            act.wait_ge(q_copied, u + 1)
                            q_head(nc.scalar, ns, 0)
                        if g == QUERY + 2:
                            q_head(nc.scalar, ns, 1)
                            q_head(nc.scalar, ns, 3).then_inc(q_spread, 1)
            clear(sems)

        OUTS = STREAMS * STORE
        with nc.Fori(0, STEPS // ROUNDS) as turn:
            pass_chunks(turn * (ROUNDS * STEP), turn * (ROUNDS * OUTS), ROUNDS)
        if STEPS % ROUNDS:
            done = STEPS - STEPS % ROUNDS
            pass_chunks(done * STEP, done * OUTS, STEPS % ROUNDS)

        with nc.Block() as block:
            @block.tensor
            def _(pe):
                pe_turn_sums(pe)
                pe.wait_ge(widened, 1)
                pe_turn_back(pe)
                pe.wait_ge(normed, 1)
                pe_project(pe, STREAMS - 1, wr, LAYERS - 1, res_done)

            @block.vector
            def _(dve):
                dve.wait_ge(sums_turned, 1)
                dve_recip(dve)
                dve.wait_ge(recip_back, 1)
                dve_norm(dve)
                dve.wait_ge(normed, 1)
                dve.wait_ge(res_done, 1)
                dve_add(dve)

            @block.scalar
            def _(act):
                act.wait_ge(recip_done, 1)
                act_widen(act)
                act.wait_ge(res_added, 1)
                act.wait_ge(stored, STEPS * OUTS + STORE)
                act_relu(act, STREAMS - 1, True)

            @block.sync
            def _(sp):
                store_out(sp, STEPS * STEP)
                sp.wait_ge(hi_ready, 1)
                store_out(sp, STEPS * STEP + CHUNK)
                sp.wait_ge(stored, STEPS * OUTS + 2 * STORE)


def finish_stage(nc, a, out, lin_sum, dnn_sum, att_sum, ident, TILES):
    with ExitStack() as ctx:
        sb = lambda name, shape: ctx.enter_context(nc.sbuf_tensor(name, shape, F32))
        sem = lambda name: ctx.enter_context(nc.semaphore(name))
        bias = sb("bias3", [P, 3])
        bias_sum = sb("bias_sum", [P, 1])
        y = sb("y", [P, TILES])
        yT = sb("yT", [TILES, P])
        ps = ctx.enter_context(nc.psum_tensor("ps_y", [TILES, P], F32))
        bias_in = sem("bias_in")
        step = sem("sum_step")
        y_turned = sem("y_turned")
        y_ready = sem("y_ready")
        y_stored = sem("y_stored")
        with nc.Block() as block:
            @block.sync
            def _(sp):
                for n, name in enumerate(("lin_b", "dnn_out_b", "att_out_b")):
                    sp.dma_start(bias[:, n:n + 1], a[name].partition_broadcast(P)).then_inc(bias_in, 16)
                sp.wait_ge(y_ready, 1)
                sp.dma_start(out.rearrange("(t p) -> t p", p=P), yT[:]).then_inc(y_stored, 16)
                sp.wait_ge(y_stored, 16)

            @block.vector
            def _(dve):
                dve.wait_ge(bias_in, 48)
                nc.vector.tensor_reduce(bias_sum[:], bias[:], AX_X, ALU.add).then_inc(step, 1)
                nc.vector.tensor_tensor(y[:], lin_sum[:], dnn_sum[:], ALU.add).then_inc(step, 1)
                dve.wait_ge(step, 2)
                nc.vector.tensor_tensor(y[:], y[:], att_sum[:], ALU.add).then_inc(step, 1)
                dve.wait_ge(step, 3)
                nc.vector.tensor_scalar(y[:], y[:], bias_sum[:, 0:1], None, ALU.add).then_inc(step, 1)

            @block.tensor
            def _(pe):
                pe.wait_ge(step, 4)
                nc.tensor.transpose(ps[:], y[:], ident[:]).then_inc(y_turned, 1)

            @block.scalar
            def _(act):
                act.wait_ge(y_turned, 1)
                nc.scalar.activation(yT[:], ps[:], ACT.Sigmoid).then_inc(y_ready, 1)


def lay_out(inputs):
    g = {k.replace("L0_rec_", ""): np.asarray(v) for k, v in inputs.items()}
    c = np.ascontiguousarray
    NS, ROWS, _ = g["sparse_embed"].shape
    ND = g["dense_embed"].shape[0]
    F = ND + NS
    a = {
        "dense": g["r_dense_input"], "sparse": g["r_sparse_input"],
        "table": g["sparse_embed"].reshape(NS * ROWS, E), "embed": g["dense_embed"].reshape(-1),
        "lin_w": np.pad(g["lin_w"].reshape(-1), (0, -F * E % P)).reshape(-1, P).T, "lin_b": g["lin_b"],
        "table_base": np.arange(NS, dtype=np.float32) * ROWS,
    }
    for pre, mine in (("dnn", "dnn"), ("att_dnn", "att")):
        w0 = g[f"{pre}_w0"]
        if mine == "att":
            w0 = w0.reshape(-1, F, HALVES, QUADS, D).transpose(0, 3, 4, 2, 1).reshape(-1, F * E)
        a[mine + "_w0"], a[mine + "_w1"], a[mine + "_w2"] = w0.T, g[f"{pre}_w1"].T, g[f"{pre}_w2"].T
        a[mine + "_out_w"] = g[f"{pre}_out_w"].reshape(-1, P).T
        a[mine + "_out_b"] = g[f"{pre}_out_b"]
        for n in range(3):
            a[f"{mine}_b{n}"] = g[f"{pre}_b{n}"].reshape(-1, P).T
    for name in ("att_wq", "att_wv", "att_wr"):
        w = g[name]
        t = w.reshape(LAYERS, HALVES, QUADS, D, HALVES, QUADS, D).transpose(5, 6, 0, 4, 1, 2, 3)
        t = np.broadcast_to(t[:, None, :, :, :, :, :, None, :],
                            (QUADS, LANES, D, LAYERS, HALVES, HALVES, QUADS, LANES, D))
        a[name] = t.reshape(P, -1)
    a.update(constants(F))
    return {k: c(v) for k, v in a.items()}


def kernel(**inputs):
    import concourse.bacc as bacc
    from concourse.bass_utils import run_bass_kernel_spmd

    arrays = lay_out(inputs)
    nc = bacc.Bacc("TRN2", target_bir_lowering=False, num_devices=1)
    aps = {k: nc.dram_tensor(f"in_{k}", v.shape, mybir.dt.from_np(v.dtype), kind="ExternalInput").ap()
           for k, v in arrays.items()}
    B = arrays["dense"].shape[0]
    out = nc.dram_tensor("out_y", (B,), F32, kind="ExternalOutput").ap()
    build_kernel(nc, aps, out)
    r = run_bass_kernel_spmd(nc, [{f"in_{k}": v for k, v in arrays.items()}], core_ids=[0])
    return r.results[0]["out_y"]
```
